# Optimizing a Trainium2 kernel written in Bass

```python
import numpy as np
import jax
import jax.numpy as jnp

def _softmax(x, axis=-1):
    return jax.nn.softmax(x, axis=axis)

def _gelu(x):
    return jax.nn.gelu(x, approximate=True)

def _silu(x):
    return jax.nn.silu(x)

def _sigmoid(x):
    return jax.nn.sigmoid(x)

def _layernorm(x, axis=-1, eps=1e-05):
    m = jnp.mean(x, axis=axis, keepdims=True)
    v = jnp.var(x, axis=axis, keepdims=True)
    return (x - m) / jnp.sqrt(v + eps)

def _scatter_add(tgt, idx, src, axis=0):
    return tgt.at[idx].add(src)

def _segment_sum(src, seg, n):
    return jax.ops.segment_sum(src, seg, n)
kernel_name = 'mk_hybrid_d1_jaxref_r4_35fcde'

def setup_inputs(seed: int=0):
    np.random.seed(seed)
    _w = jnp.asarray

    def _L0_attn_a_setup():
        import jax, jax.numpy as jnp
        import numpy as np
        N_EMBD = 256
        N_HEAD = 16
        HEAD_DIM = N_EMBD // N_HEAD
        LATENT_DIM = N_EMBD // 2
        B, T = (4, 512)
        key = jax.random.key(seed)
        ks = jax.random.split(key, 5)

        def init(k, fan_in, fan_out):
            bound = 1.0 / np.sqrt(fan_in)
            return jax.random.uniform(k, (fan_in, fan_out), jnp.float32, -bound, bound)
        return {'x': jax.random.normal(ks[0], (B, T, N_EMBD), jnp.float32), 'Wc_down': init(ks[1], N_EMBD, LATENT_DIM), 'Wq_up': init(ks[2], LATENT_DIM, N_EMBD), 'Wkv_up': init(ks[3], LATENT_DIM, 2 * HEAD_DIM), 'Wc_proj': init(ks[4], N_EMBD, N_EMBD)}
    _L0_attn_a_in = _L0_attn_a_setup()

    def _L0_attn_b_setup():
        import jax, jax.numpy as jnp
        import numpy as np
        import math
        NUM_HEADS = 16
        D_MODEL = 256
        B, T = (1, 1024)
        key = jax.random.key(seed)
        kx, kq, kk, kv, ko = jax.random.split(key, 5)
        s = 1.0 / math.sqrt(D_MODEL)
        return {'x': jax.random.normal(kx, (B, T, D_MODEL), dtype=jnp.float32), 'Wq': jax.random.normal(kq, (D_MODEL, D_MODEL), dtype=jnp.float32) * s, 'Wk': jax.random.normal(kk, (D_MODEL, D_MODEL), dtype=jnp.float32) * s, 'Wv': jax.random.normal(kv, (D_MODEL, D_MODEL), dtype=jnp.float32) * s, 'Wo': jax.random.normal(ko, (D_MODEL, D_MODEL), dtype=jnp.float32) * s}
    _L0_attn_b_in = _L0_attn_b_setup()

    def _L0_ffn_setup():
        import jax, jax.numpy as jnp
        import numpy as np
        from jax import lax
        T, B, I, M, O = (64, 64, 256, 256, 256)

        def _xavier(key, shape):
            fan_out, fan_in = shape
            limit = float(np.sqrt(6.0 / (fan_in + fan_out)))
            return jax.random.uniform(key, shape, jnp.float32, -limit, limit)
        key = jax.random.key(seed)
        ks = jax.random.split(key, 9)
        x = jax.random.normal(ks[0], (T, B, I), jnp.float32)
        return {'x': x, 'wf': _xavier(ks[1], (M, I)), 'uf': _xavier(ks[2], (M, M)), 'bf': jnp.zeros((M,), jnp.float32), 'wi': _xavier(ks[3], (M, I)), 'ui': _xavier(ks[4], (M, M)), 'bi': jnp.zeros((M,), jnp.float32), 'wc': _xavier(ks[5], (M, I)), 'uc': _xavier(ks[6], (M, M)), 'bc': jnp.zeros((M,), jnp.float32), 'wo': _xavier(ks[7], (O, I)), 'uo': _xavier(ks[8], (O, M)), 'bo': jnp.zeros((O,), jnp.float32), 'in_c': jnp.zeros((M,), jnp.float32)}
    _L0_ffn_in = _L0_ffn_setup()
    _d = {'L0_attn_a_x': _L0_attn_a_in['x'], 'L0_attn_a_Wc_down': _L0_attn_a_in['Wc_down'], 'L0_attn_a_Wq_up': _L0_attn_a_in['Wq_up'], 'L0_attn_a_Wkv_up': _L0_attn_a_in['Wkv_up'], 'L0_attn_a_Wc_proj': _L0_attn_a_in['Wc_proj'], 'L0_attn_b_Wq': _L0_attn_b_in['Wq'], 'L0_attn_b_Wk': _L0_attn_b_in['Wk'], 'L0_attn_b_Wv': _L0_attn_b_in['Wv'], 'L0_attn_b_Wo': _L0_attn_b_in['Wo'], 'L0_ffn_wf': _L0_ffn_in['wf'], 'L0_ffn_uf': _L0_ffn_in['uf'], 'L0_ffn_bf': _L0_ffn_in['bf'], 'L0_ffn_wi': _L0_ffn_in['wi'], 'L0_ffn_ui': _L0_ffn_in['ui'], 'L0_ffn_bi': _L0_ffn_in['bi'], 'L0_ffn_wc': _L0_ffn_in['wc'], 'L0_ffn_uc': _L0_ffn_in['uc'], 'L0_ffn_bc': _L0_ffn_in['bc'], 'L0_ffn_wo': _L0_ffn_in['wo'], 'L0_ffn_uo': _L0_ffn_in['uo'], 'L0_ffn_bo': _L0_ffn_in['bo'], 'L0_ffn_in_c': _L0_ffn_in['in_c']}
    _x0 = _d['L0_attn_a_x']
    _d['L0_attn_a_x'] = jax.random.normal(jax.random.fold_in(jax.random.key(seed), 1), (32, 512, 256), dtype=_x0.dtype)
    del _x0
    return _d

def reference(L0_attn_a_x, L0_attn_a_Wc_down, L0_attn_a_Wq_up, L0_attn_a_Wkv_up, L0_attn_a_Wc_proj, L0_attn_b_Wq, L0_attn_b_Wk, L0_attn_b_Wv, L0_attn_b_Wo, L0_ffn_wf, L0_ffn_uf, L0_ffn_bf, L0_ffn_wi, L0_ffn_ui, L0_ffn_bi, L0_ffn_wc, L0_ffn_uc, L0_ffn_bc, L0_ffn_wo, L0_ffn_uo, L0_ffn_bo, L0_ffn_in_c):

    def _L0_attn_a_ref(x, Wc_down, Wq_up, Wkv_up, Wc_proj):
        import jax, jax.numpy as jnp
        import numpy as np
        N_EMBD = 256
        N_HEAD = 16
        HEAD_DIM = N_EMBD // N_HEAD
        LATENT_DIM = N_EMBD // 2
        B, T = (4, 512)
        Bsz, Tlen, C = x.shape
        latent = x @ Wc_down
        q = (latent @ Wq_up).reshape(Bsz, Tlen, N_HEAD, HEAD_DIM)
        kv = latent @ Wkv_up
        k, v = (kv[..., :HEAD_DIM], kv[..., HEAD_DIM:])
        scale = 1.0 / np.sqrt(HEAD_DIM)
        att = jnp.einsum('bthd,bsd->bhts', q, k) * scale
        causal = jnp.tril(jnp.ones((Tlen, Tlen), dtype=bool))
        att = jnp.where(causal[None, None], att, -jnp.inf)
        att = jax.nn.softmax(att, axis=-1)
        y = jnp.einsum('bhts,bsd->bthd', att, v).reshape(Bsz, Tlen, C)
        return y @ Wc_proj

    def _L0_attn_b_ref(x, Wq, Wk, Wv, Wo):
        import jax, jax.numpy as jnp
        import numpy as np
        import math
        NUM_HEADS = 16
        D_MODEL = 256
        B, T = (1, 1024)
        Bx, Tx, D = x.shape
        H = NUM_HEADS
        dk = D // H
        q = (x @ Wq.T).reshape(Bx, Tx, H, dk)
        k = (x @ Wk.T).reshape(Bx, Tx, H, dk)
        v = (x @ Wv.T).reshape(Bx, Tx, H, dk)
        scores = jnp.einsum('bthd,bshd->bhts', q, k) / math.sqrt(dk)
        causal_mask = jnp.triu(jnp.ones((Tx, Tx), dtype=bool), k=1)
        scores = jnp.where(causal_mask, jnp.float32(-jnp.inf), scores).astype(jnp.float32)
        attn = jax.nn.softmax(scores, axis=-1)
        out = jnp.einsum('bhts,bshd->bthd', attn, v).reshape(Bx, Tx, D)
        return out @ Wo.T

    def _L0_ffn_ref(x, wf, uf, bf, wi, ui, bi, wc, uc, bc, wo, uo, bo, in_c):
        import jax, jax.numpy as jnp
        import numpy as np
        from jax import lax
        T, B, I, M, O = (64, 64, 256, 256, 256)

        def _xavier(key, shape):
            fan_out, fan_in = shape
            limit = float(np.sqrt(6.0 / (fan_in + fan_out)))
            return jax.random.uniform(key, shape, jnp.float32, -limit, limit)
        batch = x.shape[1]
        c0 = jnp.broadcast_to(in_c, (batch, in_c.shape[0]))

        def step(c, xt):
            ft = jax.nn.sigmoid(xt @ wf.T + c @ uf.T + bf)
            it = jax.nn.sigmoid(xt @ wi.T + c @ ui.T + bi)
            gt = jnp.tanh(xt @ wc.T + c @ uc.T + bc)
            c = ft * c + it * gt
            return (c, None)
        c_final, _ = lax.scan(step, c0, x)
        h = jnp.tanh(jnp.einsum('tbi,oi->tbo', x, wo) + c_final @ uo.T + bo)
        return h
    x = L0_attn_a_x
    x = x + _L0_attn_a_ref(_layernorm(x, axis=-1), L0_attn_a_Wc_down, L0_attn_a_Wq_up, L0_attn_a_Wkv_up, L0_attn_a_Wc_proj)
    x = x + _L0_ffn_ref(_layernorm(x, axis=-1), L0_ffn_wf, L0_ffn_uf, L0_ffn_bf, L0_ffn_wi, L0_ffn_ui, L0_ffn_bi, L0_ffn_wc, L0_ffn_uc, L0_ffn_bc, L0_ffn_wo, L0_ffn_uo, L0_ffn_bo, L0_ffn_in_c)
    x = x + _L0_attn_b_ref(_layernorm(x, axis=-1), L0_attn_b_Wq, L0_attn_b_Wk, L0_attn_b_Wv, L0_attn_b_Wo)
    x = x + _L0_ffn_ref(_layernorm(x, axis=-1), L0_ffn_wf, L0_ffn_uf, L0_ffn_bf, L0_ffn_wi, L0_ffn_ui, L0_ffn_bi, L0_ffn_wc, L0_ffn_uc, L0_ffn_bc, L0_ffn_wo, L0_ffn_uo, L0_ffn_bo, L0_ffn_in_c)
    return x

_drawn_inputs = setup_inputs


def setup_inputs(seed=0):
    import zlib

    import numpy as np

    out = dict(_drawn_inputs(seed))
    spreads = {'L0_ffn_bf': (0.0, 0.467),
     'L0_ffn_bi': (0.0, 0.458),
     'L0_ffn_bc': (0.0, 0.1),
     'L0_ffn_bo': (0.0, 0.1),
     'L0_ffn_in_c': (0.0, 0.8)}
    factors = {'L0_attn_a_Wq_up': 8.0}
    for name, (base, spread) in spreads.items():
        noise = np.random.default_rng([zlib.crc32(name.encode()), seed]).standard_normal(out[name].shape)
        drawn = base * np.exp(spread * noise) if base else spread * noise
        out[name] = jnp.asarray(drawn.astype(out[name].dtype))
    for name, factor in factors.items():
        out[name] = (out[name] * factor).astype(out[name].dtype)
    return out
```

```python
from contextlib import ExitStack

from concourse import mybir

ALU = mybir.AluOpType
ACT = mybir.ActivationFunctionType
AX = mybir.AxisListType
F32 = mybir.dt.float32
F32R = mybir.dt.float32r
BF16 = mybir.dt.bfloat16
I32 = mybir.dt.int32

P = 128
NB = 32
T = 512
C = 256
KC = C // P
TB = T // P
H = 16
D = C // H
SCALE = 0.25
EPS = 1e-5
NEG = -1e30
BIG = 3e38
Q_PARTS = (0, 1, 2, 0, 1, 0)
K_PARTS = (2, 1, 0, 1, 0, 0)
Q_RUNS = ((0, 0, 3), (3, 0, 2), (5, 0, 1))
K_RUNS = ((0, 0, 3), (3, 1, 2), (5, 2, 1))
ROWS = D * len(Q_PARTS)
STACK = ROWS + 2

W_DOWN_Q, W_KV, W_PROJ = 0, 1, 2
W_F, U_F, W_I, U_I, W_G, U_G, W_O, U_O = range(3, 11)
W_BQ, W_BK, W_BV, W_BO = range(11, 15)
NW = 15
GATES = ((W_F, U_F), (W_I, U_I), (W_G, U_G))

EXP_UNITS = [((j,), 0, 512) for j in range(4)] + [((j,), 1, 384) for j in range(4)] + \
            [((0, 1), 2, 256), ((2, 3), 2, 256), ((0, 1, 2, 3), 3, 128)]
MAX_UNITS = [((j,), 3, 512) for j in range(4)] + [((j,), 2, 384) for j in range(4)] + \
            [((0, 1), 1, 256), ((2, 3), 1, 256), ((0, 1, 2, 3), 0, 128)]
NU = len(EXP_UNITS)
UA = 4 * NU
UH = 2 * NU
EXP_BANKS, MAX_BANKS, P_BUFS, PV_LAG = 3, 2, 5, 3
LN_OPS = TB + 3 + 3 + 2 + 9 + TB

MAX0, MAX1 = ["m00", "m01"], ["m10", "m11"]
EVENTS = {
    "A": {16: ["y0"], 21: MAX1 + ["xT0", "xT1"], 24: ["lat"], 27: ["y1"], 29: ["q0", "q1"], 31: ["kv"],
          38: ["y2"]},
    "B": {16: ["y0"], 21: MAX1 + ["xT0", "xT1"], 23: ["h0", "h1"], 27: ["y1"], 33: ["x2T0", "x2T1"],
          36: ["q0", "q1"], 38: ["y2"], 40: ["k0", "k1"]},
}
VALUES = ["v0", "v1"]
POST = ["yT0", "yT1", "o0", "o1"]
STEP = ["sT0", "sT1", "g0", "g1", "g2", "g3", "g4", "g5"]
BIAS = ["b0", "b1"]
OUTC = ["cT00", "cT01", "cT10", "cT11", "ch00", "ch01", "ch10", "ch11"]
MAX0_AT = {"o1": range(0, 6), "g0": range(6, 11), "g1": range(11, 15), "g2": range(15, 19), "g3": range(19, 22)}
UNIT_OF = {"q0": 0, "q1": 1, "kv": 2, "k0": 2, "k1": 3}


def prep_uses(name):
    return [use for u in sorted(EVENTS[name]) for use in EVENTS[name][u] if use[0] not in "ym"]


ORDER = {"C": OUTC}
for _ph in "AB":
    ORDER[_ph + "pro"] = prep_uses(_ph) + VALUES + MAX0
    ORDER[_ph + "body"] = [use for u in sorted(EVENTS[_ph]) for use in EVENTS[_ph][u]] + ["y3"] + VALUES + \
        POST + STEP[:-1] + MAX0 + STEP[-1:]
    ORDER[_ph + "bias"] = BIAS

RATES = {
    "x_loaded": ("P", 16, 16), "ln_x": ("P", LN_OPS, LN_OPS), "ln_x2": ("P", 0, LN_OPS),
    "high_p": ("P", 3, 4), "part1": ("P", 3, 4), "part2": ("P", 3, 4), "part3": ("P", 3, 4),
    "kv_copied": ("P", 1, 0),
    "written0": ("P", 48, 96), "written1": ("P", 48, 96),
    "stacked0": ("P", 48, 96), "stacked1": ("P", 48, 96), "k_stacked": ("P", 96, 0),
    "h_tanh": ("P", 0, 2), "x2_sum": ("P", 0, 2),
    "m_high0": ("P", 2, 2), "m_high1": ("A", 2, 2), "m_loaded0": ("P", 32, 32), "m_loaded1": ("A", 32, 32),
    "scores_full": ("A", UA, UA), "exp_done": ("A", UA, UA), "masked": ("A", UA, UA), "pv_done": ("A", UA, UA),
    "y_copied": ("A", 4, 4), "inv_sum": ("A", 4, 4), "high_a": ("A", 4, 4),
    "xres_copied": ("A", 16, 16), "x_stored": ("A", 16, 16), "ln_a": ("A", LN_OPS, LN_OPS),
    "c_sum": ("A", 3, 3), "c_new": ("A", 2, 2), "c_low": ("A", 1, 1),
    "max_full": ("M", UA, UA), "max_taken": ("M", UA, UA),
}


class Pass:

    def __init__(self, name):
        self.name = name
        self.shared = name == "A"
        self.events = EVENTS[name]
        self.prep = prep_uses(name)
        self.units = 3 if self.shared else 4

    def val(self, sem, n, k):
        kind, ra, rb = RATES[sem]
        rate, base = (ra, 0) if self.shared else (rb, ra * {"P": NB + 1, "A": NB, "M": NB}[kind])
        if kind == "M" and not self.shared:
            base += UH
        return n * rate + (base + k) if rate else base + k


class Work:

    def __init__(self, key, it=0):
        self.order, self.base, self.it = ORDER[key], BASE[key], it

    def slot(self, use):
        return self.order.index(use) % 2

    def count(self, k):
        return self.it * (len(self.order) // 2) + (self.base + k)

    def nth(self, use):
        return self.order.index(use) // 2


BASE, _at = {}, 0
for _key, _times in (("Apro", 1), ("Abody", NB), ("Abias", 1), ("Bpro", 1), ("Bbody", NB), ("Bbias", 1),
                     ("C", NB // 2)):
    assert len(ORDER[_key]) % 2 == 0
    BASE[_key] = _at
    _at += _times * len(ORDER[_key]) // 2


def build(nc, x, wts, cols, bo_rows, out):
    ctx = ExitStack()
    with ctx:
        def sb(name, shape, dt=F32):
            return ctx.enter_context(nc.sbuf_tensor(name, shape, dt))

        def sem(name):
            return ctx.enter_context(nc.semaphore(name))

        x1_dram = nc.dram_tensor("x1_dram", (NB, T, C), F32, kind="Internal").ap()
        x3_dram = nc.dram_tensor("x3_dram", (NB, T, C), F32, kind="Internal").ap()

        scratch = nc.dram_tensor("scratch", (2, 2, 3, D, 8, T), BF16, kind="Internal").ap()

        def tokens(a):
            return a.rearrange("b (t p) c -> b p t c", p=P)

        x_v, x1_v, x3_v, out_v = tokens(x), tokens(x1_dram), tokens(x3_dram), tokens(out)

        wh = sb("wh", [P, NW, 512], F32R)
        wl = sb("wl", [P, NW, 512], F32R)
        x_in = sb("x_in", [P, TB, C])
        x_res = sb("x_res", [P, TB, C])
        xn = sb("xn", [P, TB, C])
        xT_h = sb("xT_h", [P, KC, T], F32R)
        xT_l = sb("xT_l", [P, KC, T], F32R)
        lat_h = sb("lat_h", [P, T], F32R)
        lat_l = sb("lat_l", [P, T], F32R)
        part = [sb(f"part{i}", [P, 4, T], BF16) for i in range(3)]
        rest = sb("rest", [P, 2, T])
        kv_sb = sb("kv_sb", [P, T])
        qs = sb("qs", [P, H, T], BF16)
        ks = sb("ks", [P, H, T], BF16)
        v_sb = sb("v_sb", [P, TB, H, 32])
        probs = sb("probs", [P, P_BUFS, 512])
        y_raw = sb("y_raw", [P, 2, T])
        tok = sb("tok", [P, TB, C])
        tT_h = sb("tT_h", [P, KC, T], F32R)
        tT_l = sb("tT_l", [P, KC, T], F32R)
        x_new = sb("x_new", [P, TB, C])
        gate = sb("gate", [P, 3, KC, T])
        cell = sb("cell", [P, KC, T])
        c_h = sb("c_h", [P, KC, T], F32R)
        c_l = sb("c_l", [P, KC, T], F32R)
        c_bias = sb("c_bias", [P, TB, C])
        neg_max = sb("neg_max", [P, TB, H])
        m_part = [sb(f"m_part{i}", [8, 2, T // 2], BF16) for i in range(2)]
        inv = sb("inv", [P, 2, TB, 4])
        stats = sb("stats", [P, TB, 6])
        ln_t = sb("ln_t", [P, 6, TB])
        ident = sb("ident", [P, P])
        ident_b = sb("ident_b", [P, P], BF16)
        neg_mask = sb("neg_mask", [P, P], BF16)
        cap = sb("cap", [P, 4, P])
        tick = sb("tick", [1, 1 + P_BUFS])
        col = sb("col", [P, 8])
        bo_sb = sb("bo_sb", [P, C])

        ps_exp = ctx.enter_context(nc.psum_tensor("ps_exp", [P, EXP_BANKS, 512], F32))
        ps_max = ctx.enter_context(nc.psum_tensor("ps_max", [P, MAX_BANKS, 512], F32))
        ps_y = ctx.enter_context(nc.psum_tensor("ps_y", [P, 512], F32))
        ps_w = ctx.enter_context(nc.psum_tensor("ps_w", [P, 2, 512], F32))

        S = {name: sem(name) for name in RATES}
        work_full = [sem(f"work_full{i}") for i in range(2)]
        work_free = [sem(f"work_free{i}") for i in range(2)]
        zeroed, consts, ident_cast = sem("zeroed"), sem("consts"), sem("ident_cast")
        w_raw = [sem(f"w_raw{i}") for i in range(6)]
        w_high, w_low = sem("w_high"), sem("w_low")
        small_loaded, col_half = sem("small_loaded"), sem("col_half")
        c_start = sem("c_start")
        c_loaded = [sem(f"c_loaded{i}") for i in range(2)]
        ln_c = [sem(f"ln_c{i}") for i in range(2)]
        high_c, tanh_c, sum_c = sem("high_c"), sem("tanh_c"), sem("sum_c")
        out_stored = [sem(f"out_stored{i}") for i in range(2)]

        gate_tok = gate[:, 0, :, :].rearrange("p k (a c) -> p (k a) c", c=C)
        x_c, norm_c, h_c = (x_in, x_res), (xn, tok), (x_new[:, :, :], gate_tok)
        turned_c = ((xT_h, xT_l), (tT_h, tT_l))

        block = ctx.enter_context(nc.Block())

        def wait(eng, ph, name, n, k):
            value = ph.val(name, n, k)
            if isinstance(value, int) and value == 0:
                return
            eng.wait_ge(S[name], value)

        def wait_full(eng, w, use):
            eng.wait_ge(work_full[w.slot(use)], w.count(w.nth(use) + 1))

        def wait_read(eng, w, *uses, bank_of=None):
            need = {}
            for use in uses:
                need[w.slot(use)] = max(need.get(w.slot(use), 0), w.nth(use) + 1)
            if bank_of:
                need[w.slot(bank_of)] = max(need.get(w.slot(bank_of), 0), w.nth(bank_of))
            for slot, k in need.items():
                value = w.count(k)
                if not (isinstance(value, int) and value == 0):
                    eng.wait_ge(work_free[slot], value)

        def wait_taken(eng, ph, n, unit):
            if unit == 2 and ph.shared:
                wait(eng, ph, "k_stacked", n, 0)
            else:
                wait(eng, ph, f"written{unit % 2}", n, 0)

        pass_a, pass_b = Pass("A"), Pass("B")

        nc.disable_value_cache = True
        @block.sync
        def _(sp):
            sp.dma_start(col[:, :], cols).then_inc(small_loaded, 16)
            sp.dma_start(bo_sb[:, :], bo_rows).then_inc(small_loaded, 16)
            for i in range(NW):
                if i >= 6:
                    sp.wait_ge(w_low, i - 5)
                sp.dma_start(gate[:, (i % 6) // 2, i % 2, :], wts[i]).then_inc(w_raw[i % 6], 16)

            def load(ph, b):
                sp.dma_start(x_in[:, :, :], (x_v if ph.shared else x1_v)[b]).then_inc(S["x_loaded"], 16)

            def write_half(ph, n, half):
                wait(sp, ph, f"stacked{half}", n, 0)
                for k in range(1 if ph.shared else 2):
                    unit = half + 2 * k
                    wait(sp, ph, "part3", n, unit + 1)
                    for i in range(3):
                        sp.dma_start(scratch[half, k, i if k == 0 else 2 - i].rearrange("d g n -> g d n"),
                                     part[i][:, unit, :]).then_inc(S[f"written{half}"], 16)

            def stack_half(ph, n, half):
                wait(sp, ph, f"written{half}", n, 48 if ph.shared else 96)
                for k, (dst, runs) in enumerate(((qs, Q_RUNS), (ks, K_RUNS))[:1 if ph.shared else 2]):
                    for at, first, blocks in runs:
                        sp.dma_start(dst[D * at:D * (at + blocks), 8 * half:8 * half + 8, :],
                                     scratch[half, k, first:first + blocks].rearrange("j d g n -> (j d) g n"))\
                            .then_inc(S[f"stacked{half}"], 16)

            def stack_shared_k(ph, n):
                wait(sp, ph, "part3", n, 3)
                for j, i in enumerate(K_PARTS):
                    sp.dma_start(ks[D * j:D * j + D, 0, :], part[i][0:D, 2, :]).then_inc(S["k_stacked"], 16)

            def max_rows(ph, n, half, w, uses):
                wait_read(sp, w, *uses)
                for i in range(2):
                    sp.dma_start(qs[ROWS + i:ROWS + i + 1, 8 * half:8 * half + 8, :],
                                 m_part[i][:, :, :]).then_inc(S[f"m_loaded{half}"], 16)

            def body(ph, t, n, b):
                w = Work(ph.name + "body", t)
                if not ph.shared:
                    wait(sp, ph, "x2_sum", t, 2)
                wait(sp, ph, "ln_a", t, 0)
                wait(sp, ph, "x_loaded", t, 16)
                sp.dma_start(x_res[:, :, :], x_in[:, :, :]).then_inc(S["xres_copied"], 16)
                wait(sp, ph, "xres_copied", t, 16)
                wait(sp, ph, "ln_x", t, LN_OPS)
                if not ph.shared:
                    wait(sp, ph, "ln_x2", t, LN_OPS)
                load(ph, b)
                max_rows(ph, t, 1, w, MAX1)
                write_half(ph, n, 0)
                wait(sp, ph, "scores_full", t, UH)
                stack_half(ph, n, 0)
                write_half(ph, n, 1)
                wait(sp, ph, "scores_full", t, UA)
                if ph.shared:
                    stack_shared_k(ph, n)
                stack_half(ph, n, 1)
                wait_read(sp, w, "o0", "o1")
                sp.dma_start((x1_v if ph.shared else x3_v)[t], x_new[:, :, :]).then_inc(S["x_stored"], 16)
                max_rows(ph, n, 0, w, MAX0)

            for ph in (pass_a, pass_b):
                if ph is pass_b:
                    wait(sp, pass_a, "x_stored", NB - 1, 16)
                    wait(sp, pass_a, "ln_x", NB, LN_OPS)
                load(ph, 0)
                if ph.shared:
                    stack_shared_k(ph, 0)
                for half in range(2):
                    write_half(ph, 0, half)
                for half in range(2):
                    stack_half(ph, 0, half)
                max_rows(ph, 0, 0, Work(ph.name + "pro"), MAX0)
                with sp.Fori(0, NB - 1) as t:
                    body(ph, t, t + 1, t + 1)
                body(ph, NB - 1, NB, NB - 1)

            wait(sp, pass_b, "x_stored", NB - 1, 16)
            wait(sp, pass_b, "ln_x2", NB, LN_OPS)
            wait(sp, pass_b, "ln_a", NB - 1, LN_OPS)
            with sp.Fori(0, NB // 2) as t:
                for i in range(2):
                    sp.wait_ge(sum_c, 4 * t)
                    sp.dma_start(x_c[i][:, :, :], x3_v[2 * t + i]).then_inc(c_loaded[i], 16)
                for i in range(2):
                    sp.wait_ge(sum_c, 4 * t + (2 * i + 2))
                    sp.dma_start(out_v[2 * t + i], h_c[i]).then_inc(out_stored[i], 16)
            for i in range(2):
                sp.wait_ge(out_stored[i], 16 * (NB // 2))
            wait(sp, pass_b, "m_loaded0", NB, 32)

        nc.disable_value_cache = False
        @block.gpsimd
        def _(pool):
            pool.memset(ident[:, :], 0.0).then_inc(zeroed, 1)
            pool.memset(neg_mask[:, :], 0.0).then_inc(zeroed, 1)
            pool.memset(cap[:, :, :], BIG).then_inc(zeroed, 1)
            pool.memset(tick[:, :], 0.0)
            pool.memset(v_sb[:, :, :, :], 0.0).then_inc(zeroed, 1)
            pool.wait_ge(zeroed, 4)
            pool.memset(ks[ROWS:P, :, :], 1.0).then_inc(consts, 1)
            pool.wait_ge(consts, 1)
            pool.memset(v_sb[:, :, :, D:D + 1], 1.0).then_inc(consts, 1)
            pool.affine_select(out=ident[:, :], in_=ident[:, :], compare_op=ALU.not_equal, fill=1.0,
                               base=0, pattern=[[-1, P]], channel_multiplier=1).then_inc(consts, 1)
            pool.affine_select(out=neg_mask[:, :], in_=neg_mask[:, :], compare_op=ALU.is_ge, fill=NEG,
                               base=0, pattern=[[-1, P]], channel_multiplier=1).then_inc(consts, 1)
            pool.affine_select(out=cap[:, :, :], in_=cap[:, :, :], compare_op=ALU.is_ge, fill=0.0,
                               base=0, pattern=[[0, 4], [1, P]], channel_multiplier=-1).then_inc(consts, 1)
            pool.wait_ge(consts, 5)

            def third_part(ph, n, unit):
                wait(pool, ph, "part2", n, unit + 1)
                wait_taken(pool, ph, n, unit)
                pool.tensor_tensor(part[2][:, unit, :], rest[:, unit % 2, :], part[1][:, unit, :],
                                   ALU.subtract).then_inc(S["part3"], 1)

            def mask(ph, t, u):
                heads, _, width = EXP_UNITS[u % NU]
                n = len(heads)
                wait(pool, ph, "exp_done", t, u + 1)
                at = 1 + u % P_BUFS
                pool.tensor_tensor(tick[:, at:at + 1], tick[:, 0:1], tick[:, 0:1], ALU.mult)
                pr = probs[:, u % P_BUFS, 0:n * width].rearrange("p (h n) -> p h n", h=n)[:, :, 0:P]
                pool.affine_select(out=pr, in_=pr, compare_op=ALU.is_ge, fill=0.0, base=0,
                                   pattern=[[0, n], [1, P]], channel_multiplier=-1).then_inc(S["masked"], 1)

            for ph in (pass_a, pass_b):
                for unit in range(ph.units):
                    third_part(ph, 0, unit)
                with pool.Fori(0, NB) as t:
                    for u in range(UA):
                        mask(ph, t, u)
                        for use in ph.events.get(u - 2, []):
                            if use in UNIT_OF:
                                third_part(ph, t + 1, UNIT_OF[use])

        @block.scalar
        def _(act):
            act.wait_ge(small_loaded, 32)
            act.activation(col[:, 0:4], col[:, 0:4], ACT.Copy, scale=0.5).then_inc(col_half, 1)
            act.wait_ge(col_half, 1)

            def copy_high(ph, w, use, dst, name):
                wait_full(act, w, use)
                act.activation(dst, ps_w[:, w.slot(use), :], ACT.Copy).then_inc(S[name], 1)

            def two_parts(ph, n, w, use):
                unit = UNIT_OF[use]
                wait_taken(act, ph, n, unit)
                wait_full(act, w, use)
                if use == "kv":
                    act.activation(kv_sb[:, :], ps_w[:, w.slot(use), :], ACT.Copy).then_inc(S["kv_copied"], 1)
                act.activation(part[0][:, unit, :], ps_w[:, w.slot(use), :], ACT.Copy,
                               scale=SCALE if unit < 2 else 1.0).then_inc(S["part1"], 1)
                wait_read(act, w, use)
                act.activation(part[1][:, unit, :], rest[:, unit % 2, :], ACT.Copy).then_inc(S["part2"], 1)

            def prep(ph, n, w, use):
                if "T" in use:
                    copy_high(ph, w, use, xT_h[:, int(use[-1]), :], "high_p")
                elif use == "lat":
                    copy_high(ph, w, use, lat_h[:, :], "high_p")
                elif use in ("h0", "h1"):
                    wait_read(act, w, use)
                    h = x_new[:, 2 * int(use[1]):2 * int(use[1]) + 2, :]
                    act.activation(h, h, ACT.Tanh).then_inc(S["h_tanh"], 1)
                else:
                    two_parts(ph, n, w, use)

            def values(ph, w):
                for i, use in enumerate(VALUES):
                    wait_full(act, w, use)
                    bank = ps_w[:, w.slot(use), :]
                    if ph.shared:
                        act.activation(v_sb[:, 2 * i:2 * i + 2, 0, 0:D],
                                       bank[:, 0:2 * P].rearrange("p (b n) -> p b n", b=2)[:, :, D:2 * D],
                                       ACT.Copy).then_inc(work_free[w.slot(use)], 1)
                    else:
                        act.activation(v_sb[:, 2 * i:2 * i + 2, :, 0:D].rearrange("p b h d -> p (b h) d"),
                                       bank.rearrange("p (g d) -> p g d", d=D),
                                       ACT.Copy).then_inc(work_free[w.slot(use)], 1)

            def max_high(ph, n, half, w, uses):
                for i, use in enumerate(uses):
                    wait(act, ph, f"m_loaded{1 - half}", n, 32 if half else 0)
                    wait_full(act, w, use)
                    act.activation(m_part[0][:, i, :], ps_w[0:8, w.slot(use), 0:T // 2], ACT.Copy)\
                        .then_inc(S[f"m_high{half}"], 1)

            def exps(ph, t, u):
                heads, _, width = EXP_UNITS[u % NU]
                used = len(heads) * width
                wait(act, ph, "pv_done", t, max(0, u - P_BUFS + 1))
                wait(act, ph, "scores_full", t, u + 1)
                act.activation(probs[:, u % P_BUFS, 0:used], ps_exp[:, u % EXP_BANKS, 0:used], ACT.Exp)\
                    .then_inc(S["exp_done"], 1)

            def copy_y(ph, t, g):
                wait(act, ph, "pv_done", t, NU * (g + 1))
                act.activation(y_raw[:, g % 2, :], ps_y[:, :], ACT.Copy).then_inc(S["y_copied"], 1)

            def gates(ph, t, w, i):
                g, m = divmod(i, KC)
                wait(act, ph, "c_sum", t, 0)
                wait_full(act, w, f"g{i}")
                act.activation(gate[:, g, m, :], ps_w[:, w.slot(f"g{i}"), :], ACT.Tanh,
                               bias=col[:, 2 * g + m:2 * g + m + 1], scale=0.5 if g < 2 else 1.0)\
                    .then_inc(work_free[w.slot(f"g{i}")], 1)

            for ph in (pass_a, pass_b):
                w = Work(ph.name + "pro")
                for use in ph.prep:
                    prep(ph, 0, w, use)
                values(ph, w)
                max_high(ph, 0, 0, w, MAX0)
                with act.Fori(0, NB) as t:
                    w = Work(ph.name + "body", t)
                    for u in range(UA):
                        exps(ph, t, u)
                        if u % NU == PV_LAG and u > NU:
                            copy_y(ph, t, u // NU - 1)
                        if u == UH - 1:
                            max_high(ph, t, 1, w, MAX1)
                        for use in ph.events.get(u, []):
                            if use in ph.prep:
                                prep(ph, t + 1, w, use)
                    copy_y(ph, t, 3)
                    values(ph, w)
                    for use in ("yT0", "yT1", "sT0", "sT1"):
                        copy_high(ph, w, use, tT_h[:, int(use[-1]), :], "high_a")
                    for i in range(5):
                        gates(ph, t, w, i)
                    max_high(ph, t + 1, 0, w, MAX0)
                    gates(ph, t, w, 5)
                    wait(act, ph, "c_sum", t, 3)
                    act.activation(cell[:, :, :], gate[:, 1, :, :], ACT.Copy, scale=0.5).then_inc(S["c_new"], 1)
                    act.activation(c_h[:, :, :], gate[:, 1, :, :], ACT.Copy, scale=0.5).then_inc(S["c_new"], 1)

            with act.Fori(0, NB // 2) as t:
                w = Work("C", t)
                for i in range(2):
                    for k in range(KC):
                        wait_full(act, w, f"cT{i}{k}")
                        act.activation(turned_c[i][0][:, k, :], ps_w[:, w.slot(f"cT{i}{k}"), :], ACT.Copy)\
                            .then_inc(high_c, 1)
                for i in range(2):
                    for half in range(2):
                        wait_read(act, w, f"ch{i}{half}")
                        h = h_c[i][:, 2 * half:2 * half + 2, :]
                        act.activation(h, h, ACT.Tanh).then_inc(tanh_c, 1)

        @block.vector
        def _(dve):
            for i in range(NW):
                dve.wait_ge(w_raw[i % 6], 16 * (i // 6 + 1))
                raw = gate[:, (i % 6) // 2, i % 2, :]
                dve.tensor_copy(wh[:, i, :], raw).then_inc(w_high, 1)
                dve.wait_ge(w_high, i + 1)
                dve.tensor_tensor(wl[:, i, :], raw, wh[:, i, :].bitcast(F32), ALU.subtract).then_inc(w_low, 1)
            dve.wait_ge(consts, 5)
            dve.tensor_copy(ident_b[:, :], ident[:, :]).then_inc(ident_cast, 1)
            dve.wait_ge(small_loaded, 32)

            def first_state(n):
                done = 5 * n
                dve.memset(cell[:, :, :], 0.0).then_inc(c_start, 1)
                dve.wait_ge(c_start, done + 1)
                for m in range(KC):
                    dve.tensor_scalar(cell[:, m, :], cell[:, m, :], col[:, 6 + m:7 + m], None, ALU.add)\
                        .then_inc(c_start, 1)
                dve.wait_ge(c_start, done + 3)
                dve.tensor_copy(c_h[:, :, :], cell[:, :, :]).then_inc(c_start, 1)
                dve.wait_ge(c_start, done + 4)
                dve.tensor_tensor(c_l[:, :, :], cell[:, :, :], c_h[:, :, :].bitcast(F32), ALU.subtract)\
                    .then_inc(c_start, 1)

            def layer_norm(src, dst, s, count):
                a, v, y, mean = ln_t[:, 0, :], ln_t[:, 1, :], ln_t[:, 2, :], ln_t[:, 3, :]
                diff, m2 = ln_t[:, 4, :], ln_t[:, 5, :]
                for b in range(TB):
                    dve.bn_stats(stats[:, b, :], src[:, b, :]).then_inc(s, 1)
                dve.wait_ge(s, count(TB))
                dve.tensor_tensor(mean, stats[:, :, 1], stats[:, :, 4], ALU.add).then_inc(s, 1)
                dve.tensor_tensor(diff, stats[:, :, 1], stats[:, :, 4], ALU.subtract).then_inc(s, 1)
                dve.tensor_tensor(m2, stats[:, :, 2], stats[:, :, 5], ALU.add).then_inc(s, 1)
                dve.wait_ge(s, count(TB + 3))
                dve.scalar_tensor_tensor(out=a, in0=diff, scalar=0.25, in1=diff, op0=ALU.mult, op1=ALU.mult)\
                    .then_inc(s, 1)
                dve.tensor_scalar(v, m2, 1.0 / C, EPS, ALU.mult, ALU.add).then_inc(s, 1)
                dve.tensor_scalar(mean, mean, 0.5, None, ALU.mult).then_inc(s, 1)
                dve.wait_ge(s, count(TB + 6))
                dve.tensor_tensor(v, v, a, ALU.add).then_inc(s, 1)
                dve.wait_ge(s, count(TB + 7))
                dve.tensor_scalar(y.bitcast(I32), v.bitcast(I32), -0.5, 1597463007.0, ALU.mult, ALU.add)\
                    .then_inc(s, 1)
                for r in range(3):
                    k = TB + 8 + 3 * r
                    dve.wait_ge(s, count(k))
                    dve.tensor_tensor(a, y, y, ALU.mult).then_inc(s, 1)
                    dve.wait_ge(s, count(k + 1))
                    dve.scalar_tensor_tensor(out=a, in0=a, scalar=-0.5, in1=v, op0=ALU.mult, op1=ALU.mult)\
                        .then_inc(s, 1)
                    dve.wait_ge(s, count(k + 2))
                    dve.scalar_tensor_tensor(out=y, in0=a, scalar=1.5, in1=y, op0=ALU.add, op1=ALU.mult)\
                        .then_inc(s, 1)
                dve.wait_ge(s, count(TB + 17))
                for b in range(TB):
                    dve.tensor_scalar(dst[:, b, :], src[:, b, :], mean[:, b:b + 1], y[:, b:b + 1],
                                      ALU.subtract, ALU.mult).then_inc(s, 1)

            def low(ph, w, use, dst, high, name, n, k):
                wait(dve, ph, name, n, k)
                dve.tensor_tensor(dst, ps_w[:, w.slot(use), :], high.bitcast(F32), ALU.subtract)\
                    .then_inc(work_free[w.slot(use)], 1)

            def take_max(ph, n, half, u):
                heads, qb, width = MAX_UNITS[u % NU]
                h0 = 8 * half + 4 * (u // NU) + heads[0]
                k = len(heads)
                wait(dve, ph, "max_full", n, half * UH + u + 1)
                dve.tensor_reduce(neg_max[:, qb, h0:h0 + k],
                                  ps_max[:, u % MAX_BANKS, 0:k * width].rearrange("p (h n) -> p h n", h=k),
                                  AX.X, ALU.max, negate=True).then_inc(S["max_taken"], 1)

            def max_low(ph, n, half, w, uses):
                for i, use in enumerate(uses):
                    wait(dve, ph, f"m_high{half}", n, i + 1)
                    dve.tensor_tensor(m_part[1][:, i, :], ps_w[0:8, w.slot(use), 0:T // 2],
                                      m_part[0][:, i, :], ALU.subtract).then_inc(work_free[w.slot(use)], 1)

            def ln_x(ph, n):
                wait(dve, ph, "x_loaded", n, 16)
                layer_norm(x_in, xn, S["ln_x"], lambda k: ph.val("ln_x", n, k))

            def prep(ph, n, w, use):
                if "T" in use:
                    k = int(use[-1])
                    at = k + (2 if use[:2] == "x2" else 0)
                    low(ph, w, use, xT_l[:, k, :], xT_h[:, k, :], "high_p", n, at + 1)
                elif use == "lat":
                    low(ph, w, use, lat_l[:, :], lat_h[:, :], "high_p", n, 3)
                elif use in ("h0", "h1"):
                    i = int(use[1])
                    wait_full(dve, w, use)
                    dve.tensor_tensor(x_new[:, 2 * i:2 * i + 2, :].rearrange("p b c -> p (b c)"),
                                      ps_w[:, w.slot(use), :],
                                      c_bias[:, 2 * i:2 * i + 2, :].rearrange("p b c -> p (b c)"), ALU.add)\
                        .then_inc(work_free[w.slot(use)], 1)
                    if i == 1:
                        for j in range(2):
                            wait(dve, ph, "h_tanh", n, j + 1)
                            part_of = x_in[:, 2 * j:2 * j + 2, :]
                            dve.tensor_tensor(part_of, part_of, x_new[:, 2 * j:2 * j + 2, :], ALU.add)\
                                .then_inc(S["x2_sum"], 1)
                        wait(dve, ph, "x2_sum", n, 2)
                        layer_norm(x_in, xn, S["ln_x2"], lambda k: ph.val("ln_x2", n, k))
                else:
                    unit = UNIT_OF[use]
                    wait(dve, ph, "part1", n, unit + 1)
                    wait(dve, ph, "part3", n, max(0, unit - 1))
                    dve.scalar_tensor_tensor(out=rest[:, unit % 2, :], in0=ps_w[:, w.slot(use), :],
                                             scalar=SCALE if unit < 2 else 1.0, in1=part[0][:, unit, :],
                                             op0=ALU.mult, op1=ALU.subtract)\
                        .then_inc(work_free[w.slot(use)], 1)

            def normalise(ph, t, w, g):
                use = f"y{g}"
                wait_full(dve, w, use)
                bank = ps_w[:, w.slot(use), :].rearrange("p (b j d) -> p b j d", b=TB, j=4)
                dve.reciprocal(inv[:, g % 2, :, :], bank[:, :, :, D]).then_inc(S["inv_sum"], 1)
                wait(dve, ph, "inv_sum", t, g + 1)
                dve.tensor_tensor(tok[:, :, 64 * g:64 * g + 64].rearrange("p b (j d) -> p b j d", d=D),
                                  bank[:, :, :, 0:D], inv[:, g % 2, :, :].unsqueeze(3).to_broadcast([P, TB, 4, D]),
                                  ALU.mult).then_inc(work_free[w.slot(use)], 1)

            first_state(0)
            for ph in (pass_a, pass_b):
                w = Work(ph.name + "pro")
                ln_x(ph, 0)
                for use in ph.prep:
                    prep(ph, 0, w, use)
                for u in range(UH):
                    take_max(ph, 0, 0, u)
                max_low(ph, 0, 0, w, MAX0)
                with dve.Fori(0, NB) as t:
                    w = Work(ph.name + "body", t)
                    for u in range(UA):
                        if u < UH:
                            take_max(ph, t, 1, u)
                        if u == 12:
                            ln_x(ph, t + 1)
                        if u == UH - 1:
                            max_low(ph, t, 1, w, MAX1)
                        for use in ph.events.get(u, []):
                            if use in ph.prep:
                                if use == "h0":
                                    wait(dve, ph, "x_stored", t, 0)
                                prep(ph, t + 1, w, use)
                            elif use[0] == "y":
                                normalise(ph, t, w, int(use[1]))
                    normalise(ph, t, w, 3)
                    for k in range(KC):
                        low(ph, w, f"yT{k}", tT_l[:, k, :], tT_h[:, k, :], "high_a", t, k + 1)
                    wait(dve, ph, "xres_copied", t, 16)
                    wait(dve, ph, "x_stored", t, 0)
                    for i in range(2):
                        wait_full(dve, w, f"o{i}")
                        dve.tensor_tensor(x_new[:, 2 * i:2 * i + 2, :].rearrange("p b c -> p (b c)"),
                                          ps_w[:, w.slot(f"o{i}"), :],
                                          x_res[:, 2 * i:2 * i + 2, :].rearrange("p b c -> p (b c)"), ALU.add)\
                            .then_inc(work_free[w.slot(f"o{i}")], 1)
                    wait_read(dve, w, "o0", "o1")
                    layer_norm(x_new, tok, S["ln_a"], lambda k: ph.val("ln_a", t, k))
                    for use in ["o1"] + STEP[:-1]:
                        if use[0] == "s":
                            k = int(use[-1])
                            low(ph, w, use, tT_l[:, k, :], tT_h[:, k, :], "high_a", t, k + 3)
                        for u in MAX0_AT.get(use, ()):
                            take_max(ph, t + 1, 0, u)
                    max_low(ph, t + 1, 0, w, MAX0)
                    wait_read(dve, w, "g4", "g5")
                    wait(dve, ph, "c_new", t, 0)
                    flat = [gate[:, g, :, :].rearrange("p k n -> p (k n)") for g in range(3)]
                    cell_f = cell[:, :, :].rearrange("p k n -> p (k n)")
                    dve.scalar_tensor_tensor(out=flat[0], in0=flat[0], scalar=1.0, in1=cell_f,
                                             op0=ALU.add, op1=ALU.mult).then_inc(S["c_sum"], 1)
                    dve.scalar_tensor_tensor(out=flat[1], in0=flat[1], scalar=1.0, in1=flat[2],
                                             op0=ALU.add, op1=ALU.mult).then_inc(S["c_sum"], 1)
                    wait(dve, ph, "c_sum", t, 2)
                    dve.tensor_tensor(flat[1], flat[0], flat[1], ALU.add).then_inc(S["c_sum"], 1)
                    wait(dve, ph, "c_new", t, 2)
                    dve.tensor_tensor(c_l[:, :, :], cell[:, :, :], c_h[:, :, :].bitcast(F32), ALU.subtract)\
                        .then_inc(S["c_low"], 1)
                w = Work(ph.name + "bias")
                for i in range(2):
                    use = BIAS[i]
                    wait_full(dve, w, use)
                    for b in range(2):
                        ins = dve.tensor_tensor(c_bias[:, 2 * i + b, :], ps_w[:, w.slot(use), b * C:(b + 1) * C],
                                                bo_sb[:, :], ALU.add)
                    ins.then_inc(work_free[w.slot(use)], 1)
                wait_read(dve, w, *BIAS)
                if ph.shared:
                    first_state(1)

            with dve.Fori(0, NB // 2) as t:
                w = Work("C", t)
                for i in range(2):
                    dve.wait_ge(c_loaded[i], 16 * t + 16)
                    layer_norm(x_c[i], norm_c[i], ln_c[i], lambda k: LN_OPS * t + k)
                for i in range(2):
                    for k in range(KC):
                        use = f"cT{i}{k}"
                        dve.wait_ge(high_c, 4 * t + (2 * i + k + 1))
                        dve.tensor_tensor(turned_c[i][1][:, k, :], ps_w[:, w.slot(use), :],
                                          turned_c[i][0][:, k, :].bitcast(F32), ALU.subtract)\
                            .then_inc(work_free[w.slot(use)], 1)
                for i in range(2):
                    dve.wait_ge(out_stored[i], 16 * t)
                    for half in range(2):
                        use = f"ch{i}{half}"
                        wait_full(dve, w, use)
                        dve.tensor_tensor(h_c[i][:, 2 * half:2 * half + 2, :],
                                          ps_w[:, w.slot(use), :].rearrange("p (b c) -> p b c", c=C),
                                          c_bias[:, 2 * half:2 * half + 2, :], ALU.add)\
                            .then_inc(work_free[w.slot(use)], 1)
                for i in range(2):
                    for half in range(2):
                        dve.wait_ge(tanh_c, 4 * t + (2 * i + half + 1))
                        h = h_c[i][:, 2 * half:2 * half + 2, :]
                        dve.tensor_tensor(h, h, x_c[i][:, 2 * half:2 * half + 2, :], ALU.add).then_inc(sum_c, 1)

        @block.tensor
        def _(pe):
            pe.wait_ge(consts, 5)
            pe.wait_ge(ident_cast, 1)
            pe.wait_ge(w_low, NW)
            pe.wait_ge(c_start, 5)

            def exact(dst, terms, first=True, last=True):
                n = 3 * len(terms)
                i = 0
                for lh, ll, rh, rl in terms:
                    for a, b in ((lh, rh), (lh, rl), (ll, rh)):
                        ins = pe.matmul(dst, a, b, start=first and i == 0, stop=last and i == n - 1)
                        i += 1
                return ins

            def claim(w, use, *made):
                wait_read(pe, w, *made, bank_of=use)
                return ps_w[:, w.slot(use), :]

            def filled(ins, w, use):
                ins.then_inc(work_full[w.slot(use)], 1)

            def turn(w, use, src, k, *made):
                bank = claim(w, use, *made)
                for b in range(TB):
                    ins = pe.transpose(bank[:, b * P:(b + 1) * P], src[:, b, k * P:(k + 1) * P], ident[:, :])
                filled(ins, w, use)

            def by_token(w, use, i, hi, lo, tile, *made):
                bank = claim(w, use, *made)
                for b in range(2):
                    blk = slice((2 * i + b) * P, (2 * i + b + 1) * P)
                    ins = exact(bank[:, b * C:(b + 1) * C],
                                [(hi[:, k, blk], lo[:, k, blk], wh[:, tile, k * C:(k + 1) * C],
                                  wl[:, tile, k * C:(k + 1) * C]) for k in range(KC)])
                filled(ins, w, use)

            def by_width(w, use, m, tile, hi, lo, bank, first=True, last=True):
                cut = [slice(k * C + m * P, k * C + m * P + P) for k in range(KC)]
                return exact(bank, [(wh[:, tile, cut[k]], wl[:, tile, cut[k]], hi[:, k, :], lo[:, k, :])
                                    for k in range(KC)], first, last)

            def prep(ph, n, w, use):
                if "T" in use:
                    if use == "xT0":
                        wait(pe, ph, "ln_x", n, LN_OPS)
                    if use == "x2T0":
                        wait(pe, ph, "ln_x2", n, LN_OPS)
                    turn(w, use, xn, int(use[-1]))
                elif use == "lat":
                    bank = claim(w, use, "xT0", "xT1")
                    filled(exact(bank, [(wh[:, W_DOWN_Q, k * P:(k + 1) * P], wl[:, W_DOWN_Q, k * P:(k + 1) * P],
                                         xT_h[:, k, :], xT_l[:, k, :]) for k in range(KC)]), w, use)
                elif use in ("h0", "h1"):
                    by_token(w, use, int(use[1]), xT_h, xT_l, W_O, "xT0", "xT1")
                elif ph.shared:
                    cut = {"q0": (W_DOWN_Q, 2 * P), "q1": (W_DOWN_Q, 3 * P), "kv": (W_KV, 0)}[use]
                    ws = slice(cut[1], cut[1] + P)
                    bank = claim(w, use, "lat")
                    filled(exact(bank, [(wh[:, cut[0], ws], wl[:, cut[0], ws], lat_h[:, :], lat_l[:, :])]), w, use)
                else:
                    bank = claim(w, use, "x2T0", "x2T1")
                    filled(by_width(w, use, int(use[1]), W_BQ if use[0] == "q" else W_BK, xT_h, xT_l, bank), w, use)

            def values(ph, n, w):
                for i, use in enumerate(VALUES):
                    if ph.shared:
                        wait(pe, ph, "kv_copied", n, 1)
                        bank = claim(w, use)
                        for b in range(2):
                            blk = slice((2 * i + b) * P, (2 * i + b + 1) * P)
                            ins = pe.transpose(bank[:, b * P:(b + 1) * P], kv_sb[:, blk], ident[:, :])
                        filled(ins, w, use)
                    else:
                        by_token(w, use, i, xT_h, xT_l, W_BV)

            def scores_max(ph, n, half, u):
                heads, qb, width = MAX_UNITS[u % NU]
                if u == 0:
                    wait(pe, ph, f"stacked{half}", n, 48 if ph.shared else 96)
                    if ph.shared:
                        wait(pe, ph, "k_stacked", n, 96)
                wait(pe, ph, "max_taken", n, half * UH + max(0, u - MAX_BANKS + 1))
                for i, j in enumerate(heads):
                    head = 8 * half + 4 * (u // NU) + j
                    bank = ps_max[:, u % MAX_BANKS, i * width:(i + 1) * width]
                    pe.matmul(bank, qs[0:ROWS, head, qb * P:(qb + 1) * P],
                              ks[0:ROWS, 0 if ph.shared else head, 0:width], start=True, stop=False)
                    ins = pe.matmul(bank[:, width - P:width], ident_b[:, :], neg_mask[:, :], start=False, stop=True)
                ins.then_inc(S["max_full"], 1)

            def max_turn(ph, n, half, w, uses):
                wait(pe, ph, "max_taken", n, half * UH + UH)
                for i, use in enumerate(uses):
                    bank = claim(w, use)
                    for b in range(2):
                        ins = pe.transpose(bank[0:8, b * P:(b + 1) * P],
                                           neg_max[:, 2 * i + b, 8 * half:8 * half + 8], ident[:, :])
                    filled(ins, w, use)

            def scores_exp(ph, t, u):
                heads, kb, width = EXP_UNITS[u % NU]
                if u == 0:
                    wait(pe, ph, "m_loaded0", t, 32)
                if u == UH:
                    wait(pe, ph, "m_loaded1", t, 32)
                wait(pe, ph, "exp_done", t, max(0, u - EXP_BANKS + 1))
                for i, j in enumerate(heads):
                    head = 4 * (u // NU) + j
                    ins = pe.matmul(ps_exp[:, u % EXP_BANKS, i * width:(i + 1) * width],
                                    ks[0:STACK, 0 if ph.shared else head, kb * P:(kb + 1) * P],
                                    qs[0:STACK, head, T - width:T], start=True, stop=True)
                ins.then_inc(S["scores_full"], 1)

            def product(ph, t, u):
                g = u // NU
                heads, kb, width = EXP_UNITS[u % NU]
                if u % NU == 0:
                    wait(pe, ph, "y_copied", t, g)
                wait(pe, ph, "masked", t, u + 1)
                for i, j in enumerate(heads):
                    head = 0 if ph.shared else 4 * g + j
                    ins = pe.matmul(ps_y[32 * j:32 * j + 32, T - width:T], v_sb[:, kb, head, :],
                                    probs[:, u % P_BUFS, i * width:(i + 1) * width],
                                    start=(kb == 0), stop=(kb == TB - 1))
                ins.then_inc(S["pv_done"], 1)

            def turn_y(ph, t, w, g):
                use = f"y{g}"
                wait(pe, ph, "y_copied", t, g + 1)
                bank = claim(w, use)
                for b in range(TB):
                    ins = pe.transpose(bank[:, b * P:(b + 1) * P], y_raw[:, g % 2, b * P:(b + 1) * P], ident[:, :])
                filled(ins, w, use)

            for ph in (pass_a, pass_b):
                w = Work(ph.name + "pro")
                for use in ph.prep:
                    prep(ph, 0, w, use)
                values(ph, 0, w)
                for u in range(UH):
                    scores_max(ph, 0, 0, u)
                max_turn(ph, 0, 0, w, MAX0)
                with pe.Fori(0, NB) as t:
                    w = Work(ph.name + "body", t)
                    for u in range(UA):
                        scores_exp(ph, t, u)
                        if u < UH:
                            scores_max(ph, t, 1, u)
                        if u >= PV_LAG:
                            product(ph, t, u - PV_LAG)
                        if u == UH - 1:
                            max_turn(ph, t, 1, w, MAX1)
                        for use in ph.events.get(u, []):
                            if use in ph.prep:
                                prep(ph, t + 1, w, use)
                            elif use[0] == "y":
                                turn_y(ph, t, w, int(use[1]))
                    for u in range(UA - PV_LAG, UA):
                        product(ph, t, u)
                    turn_y(ph, t, w, 3)
                    values(ph, t + 1, w)
                    for k in range(KC):
                        turn(w, f"yT{k}", tok, k, "y3")
                    for i in range(2):
                        by_token(w, f"o{i}", i, tT_h, tT_l, W_PROJ if ph.shared else W_BO, "yT0", "yT1")
                    for use in ["o1"] + STEP:
                        if use == "sT0":
                            wait(pe, ph, "ln_a", t, LN_OPS)
                        if use[0] == "s":
                            turn(w, use, tok, int(use[-1]))
                        if use == "g0":
                            wait(pe, ph, "c_low", t, 0)
                        if use == "g5":
                            max_turn(ph, t + 1, 0, w, MAX0)
                        if use[0] == "g":
                            g, m = divmod(int(use[1]), KC)
                            bank = claim(w, use, "sT0", "sT1")
                            by_width(w, use, m, GATES[g][0], tT_h, tT_l, bank, True, False)
                            filled(by_width(w, use, m, GATES[g][1], c_h, c_l, bank, False, True), w, use)
                        for u in MAX0_AT.get(use, ()):
                            scores_max(ph, t + 1, 0, u)
                w = Work(ph.name + "bias")
                wait(pe, ph, "c_low", NB - 1, 1)
                for i, use in enumerate(BIAS):
                    by_token(w, use, i, c_h, c_l, U_O)
                wait_read(pe, w, *BIAS)
                if ph.shared:
                    pe.wait_ge(c_start, 10)

            with pe.Fori(0, NB // 2) as t:
                w = Work("C", t)
                for i in range(2):
                    pe.wait_ge(ln_c[i], LN_OPS * t + LN_OPS)
                    for k in range(KC):
                        turn(w, f"cT{i}{k}", norm_c[i], k)
                for i in range(2):
                    for half in range(2):
                        by_token(w, f"ch{i}{half}", half, turned_c[i][0], turned_c[i][1], W_O, f"cT{i}0", f"cT{i}1")


def kernel(**inputs):
    import numpy as np
    import concourse.bacc as bacc
    from concourse.bass_utils import run_bass_kernel_spmd

    def get(name):
        return np.asarray(inputs["L0_" + name])

    def tile(w):
        return w.reshape(KC, P, C).transpose(1, 0, 2).reshape(P, KC * C)

    wts = np.zeros((NW, P, 512), np.float32)
    wts[W_DOWN_Q, :, 0:2 * P] = get("attn_a_Wc_down").reshape(KC, P, P).transpose(1, 0, 2).reshape(P, 2 * P)
    wts[W_DOWN_Q, :, 2 * P:] = get("attn_a_Wq_up")
    wts[W_KV, :, 0:2 * D] = get("attn_a_Wkv_up")
    wts[W_PROJ] = tile(get("attn_a_Wc_proj"))
    for at, name in ((W_F, "ffn_wf"), (U_F, "ffn_uf"), (W_I, "ffn_wi"), (U_I, "ffn_ui"), (W_G, "ffn_wc"),
                     (U_G, "ffn_uc"), (W_O, "ffn_wo"), (U_O, "ffn_uo"), (W_BQ, "attn_b_Wq"), (W_BK, "attn_b_Wk"),
                     (W_BV, "attn_b_Wv"), (W_BO, "attn_b_Wo")):
        wts[at] = tile(get(name).T)
    cols = np.zeros((P, 8), np.float32)
    for i, name in enumerate(("ffn_bf", "ffn_bi", "ffn_bc", "ffn_in_c")):
        cols[:, 2 * i:2 * i + 2] = get(name).reshape(KC, P).T
    arrays = {
        "x": np.ascontiguousarray(get("attn_a_x")),
        "wts": wts,
        "cols": cols,
        "bo_rows": np.ascontiguousarray(np.broadcast_to(get("ffn_bo"), (P, C))),
    }
    nc = bacc.Bacc("TRN2", target_bir_lowering=False, num_devices=1)
    args = [nc.dram_tensor(name, a.shape, F32, kind="ExternalInput").ap() for name, a in arrays.items()]
    result = nc.dram_tensor("result", (NB, T, C), F32, kind="ExternalOutput").ap()
    build(nc, *args, result)
    r = run_bass_kernel_spmd(nc, [arrays], core_ids=[0])
    return r.results[0]["result"]
```

```python
from contextlib import ExitStack

from concourse import mybir

ALU = mybir.AluOpType
ACT = mybir.ActivationFunctionType
AX = mybir.AxisListType
F32 = mybir.dt.float32
F32R = mybir.dt.float32r
BF16 = mybir.dt.bfloat16
I32 = mybir.dt.int32

P = 128
NB = 32
T = 512
C = 256
KC = C // P
TB = T // P
H = 16
D = C // H
SCALE = 0.25
EPS = 1e-5
NEG = -1e30
Q_PARTS = (0, 1, 2, 0, 1, 0)
K_PARTS = (2, 1, 0, 1, 0, 0)
Q_RUNS = ((0, 0, 3), (3, 0, 2), (5, 0, 1))
K_RUNS = ((0, 0, 3), (3, 1, 2), (5, 2, 1))
ROWS = D * len(Q_PARTS)
STACK = ROWS + 2

W_DOWN_Q, W_KV, W_PROJ = 0, 1, 2
W_F, U_F, W_I, U_I, W_G, U_G, W_O, U_O = range(3, 11)
W_BQ, W_BK, W_BV, W_BO = range(11, 15)
NW = 15
GATES = ((W_F, U_F), (W_I, U_I), (W_G, U_G))

EXP_UNITS = [((j,), 0, 512) for j in range(4)] + [((j,), 1, 384) for j in range(4)] + \
            [((0, 1), 2, 256), ((2, 3), 2, 256), ((0, 1, 2, 3), 3, 128)]
MAX_UNITS = [((j,), 3, 512) for j in range(4)] + [((j,), 2, 384) for j in range(4)] + \
            [((0, 1), 1, 256), ((2, 3), 1, 256), ((0, 1, 2, 3), 0, 128)]
NU = len(EXP_UNITS)
UA = 4 * NU
UH = 2 * NU
EXP_BANKS, MAX_BANKS, P_BUFS, PV_LAG = 3, 2, 5, 3
LN_OPS = TB + 3 + 3 + 1 + 1 + TB
LN_COUNT = {"lnx": "ln_x", "ln2": "ln_x2", "post": "ln_a"}

MAX0, MAX1 = ["m00", "m01"], ["m10", "m11"]
EVENTS = {
    "A": {0: ["lat"], 2: ["q0"], 4: ["q0+", "y3", "move3"], 5: ["kv"], 6: ["kv+", "yT0", "yT1"],
          8: ["o0", "o1", "post"], 9: ["v0"], 10: ["v1"], 11: ["q1"], 12: ["q1+", "post+"], 13: ["sT0", "sT1"],
          16: ["g0-", "g0", "y0"], 18: ["move0"], 19: MAX1, 20: ["g1-", "g1", "lnx"], 23: ["g2-"],
          24: ["g2", "lnx+", "y1"], 26: ["move1"], 29: ["g3-", "g3", "c0"], 31: ["g4-", "g4"],
          35: ["g5-", "g5"], 36: ["y2", "move2"], 38: MAX0, 39: ["xT0", "xT1"], 41: ["c1", "state"]},
    "B": {0: ["x2T0", "x2T1"], 2: ["q0"], 4: ["q0+", "y3", "move3", "k0"], 6: ["k0+", "yT0"], 7: ["yT1", "q1"],
          8: ["q1+", "o0", "o1", "post"], 9: ["v0"], 10: ["v1"], 13: ["post+", "k1"],
          14: ["k1+", "sT0", "sT1"], 16: ["g0-"], 17: ["y0", "move0", "g0"], 19: MAX1, 20: ["g1-"],
          21: ["g1", "lnx"], 23: ["g2-"], 24: ["g2", "lnx+"], 25: ["xT0", "xT1"], 26: ["y1", "move1"],
          27: ["h0", "h1"], 28: ["c0"], 29: ["g3-", "ln2"], 30: ["g3"], 31: ["g4-", "g4", "ln2+"],
          37: ["y2", "move2"], 38: MAX0, 39: ["g5-", "g5"], 41: ["c1"], 42: ["state"]},
}
MAX_SLOTS = {
    "A": {5: 2, 6: 3, 7: 1, 8: 2, 10: 1, 11: 1, 13: 2, 14: 3, 15: 1, 16: 2, 17: 2, 18: 2, 25: 1, 26: 1,
          27: 2, 28: 3, 29: 2, 30: 2, 31: 2, 32: 2, 33: 2, 34: 2, 35: 2, 36: 1},
    "B": {4: 2, 6: 2, 7: 2, 8: 2, 10: 1, 11: 1, 12: 1, 13: 1, 14: 2, 16: 1, 17: 3, 18: 4, 25: 1, 26: 2,
          27: 2, 28: 2, 29: 2, 30: 1, 33: 1, 34: 3, 35: 3, 36: 4, 37: 1},
}


def max_units(name, slot):
    first = sum(k for s, k in MAX_SLOTS[name].items() if s < slot)
    return [(1, i) if i < UH else (0, i - UH) for i in range(first, first + MAX_SLOTS[name].get(slot, 0))]


LAST = ["y3", "yT0", "yT1", "o0", "o1", "post", "post+", "sT0", "sT1", "g0-", "g0", "g1-", "g1", "g2-", "g2",
        "c0", "g3-", "g3", "g4-", "g4", "g5-", "g5", "c1", "state"]
EARLY = {"A": ["lnx", "lnx+", "xT0", "xT1"], "B": ["lnx", "lnx+", "xT0", "xT1", "h0", "h1", "ln2", "ln2+"]}
LATE = {"A": ["lat", "q0", "q0+", "kv", "kv+", "v0", "v1", "q1", "q1+"],
        "B": ["x2T0", "x2T1", "q0", "q0+", "k0", "k0+", "q1", "q1+", "v0", "v1", "k1", "k1+"]}
MOVES = ["move0", "move1", "move2", "move3"]
NOT_ON_ACT = MOVES + ["c0", "c1", "state"] + [use + more for use in LN_COUNT for more in ("", "+")]
SPLIT = {"A": ["q0", "kv", "q1"], "B": ["q0", "k0", "q1", "k1"]}
UNIT_OF = {"q0": 0, "q1": 1, "kv": 2, "k0": 2, "k1": 3}
BIAS = ["b0", "b1"]
XC = 4
OUTC = [use for i in range(XC) for use in (f"cT{i}0", f"cT{i}1", f"ch{i}0", f"ch{i}1")]


def steps(name, *but):
    return {u: [use for use in uses if use not in but] for u, uses in EVENTS[name].items()}


def in_banks(uses):
    return [use.rstrip("-") for use in uses if use[-1] != "+" and (use[0] != "g" or use[-1] == "-") and
            use not in MOVES + ["post", "lnx", "ln2", "c0", "c1", "state"]]


STRETCHES = []
for _ph in "AB":
    _all = [use for u in sorted(EVENTS[_ph]) for use in EVENTS[_ph][u]]
    STRETCHES += [(_ph + "pro0", 1, EARLY[_ph] + LATE[_ph]), (_ph + "pro1", 1, EARLY[_ph] + MAX0),
                  (_ph + "first", 1, [use for use in _all if use not in LAST]),
                  (_ph + "body", NB - 1, _all),
                  (_ph + "last", 1, LAST), (_ph + "bias", 1, BIAS)]
STRETCHES.append(("C", NB // XC, OUTC))

ROUNDS = {"E": (NB + 2, 0), "L": (NB + 1, 0), "A": (NB, 0), "M": (NB, UH), "V": (NB, 3)}
RATES = {
    "x_loaded": ("E", 16, 16), "ln_x": ("E", LN_OPS, LN_OPS), "ln_x2": ("E", 0, LN_OPS),
    "high_e": ("E", 2, 2), "h_tanh": ("E", 0, 2), "x2_sum": ("E", 0, 2), "x2_stored": ("A", 0, 16),
    "high_l": ("L", 1, 2), "part1": ("L", 3, 4), "part2": ("L", 3, 4), "part3": ("L", 3, 4),
    "kv_copied": ("L", 1, 0), 
    "written0": ("L", 96, 96), "written1": ("L", 48, 96), "stacked0": ("L", 96, 96), "stacked1": ("A", 96, 96),
    "m_high0": ("L", 2, 2), "m_high1": ("A", 2, 2), "m_loaded0": ("L", 32, 32), "m_loaded1": ("A", 32, 32),
    "scores_full": ("A", UA, UA), "exp_done": ("A", UA, UA), "masked": ("A", UA, UA), "pv_done": ("A", UA, UA),
    "y_copied": ("A", 4, 4), "inv_sum": ("A", 4, 4), "high_a": ("A", 4, 4), "v_moved": ("V", 4, 4),
    "xres_loaded": ("A", 16, 16), "x_stored": ("A", 16, 16), "ln_a": ("A", LN_OPS, LN_OPS),
    "c_sum": ("A", 6, 6), "c_new": ("A", 1, 1), "c_low": ("A", 1, 1),
    "max_full": ("M", UA, UA), "max_taken": ("M", UA, UA),
}


def freed(u, buffers):
    return u - buffers + 1 if u >= buffers else max(v for v in range(UA) if v % buffers == u) + 1 - UA


class Pass:

    def __init__(self, name):
        self.name = name
        self.shared = name == "A"
        self.split = SPLIT[name]
        self.first = steps(name, *LAST, "move3")
        self.all = steps(name)

    def round(self, use, b):
        if use in LAST:
            return b - 1
        if use in EARLY[self.name]:
            return b + 2
        return b if use in ["y0", "y1", "y2", "move3"] + MAX1 else b + 1

    def val(self, sem, n, k):
        kind, ra, rb = RATES[sem]
        rounds, more = ROUNDS[kind]
        rate, base = (ra, 0) if self.shared else (rb, ra * rounds + more)
        if sem == "c_low":
            base += 1 if self.shared else 2
        return n * rate + (base + k) if rate else base + k


class Work:

    def __init__(self, key, it=0):
        self.order, self.start, self.base, self.it = ORDER[key] + (it,)

    def slot(self, use):
        return (self.start + self.order.index(use)) % 2

    def count(self, slot, k):
        return self.it * (len(self.order) // 2) + (self.base[slot] + k)

    def nth(self, use):
        return self.order.index(use) // 2


ORDER, _start, _base = {}, 0, [0, 0]
for _key, _times, _uses in STRETCHES:
    _uses = in_banks(_uses)
    assert _times == 1 or len(_uses) % 2 == 0
    ORDER[_key] = (_uses, _start, list(_base))
    for _i in range(_times * len(_uses)):
        _base[(_start + _i) % 2] += 1
    _start = (_start + _times * len(_uses)) % 2


def build(nc, x, wts, cols, bo_rows, out):
    ctx = ExitStack()
    with ctx:
        def sb(name, shape, dt=F32):
            return ctx.enter_context(nc.sbuf_tensor(name, shape, dt))

        def sem(name):
            return ctx.enter_context(nc.semaphore(name))

        x1_dram = nc.dram_tensor("x1_dram", (NB, T, C), F32, kind="Internal").ap()
        x3_dram = nc.dram_tensor("x3_dram", (NB, T, C), F32, kind="Internal").ap()

        scratch = nc.dram_tensor("scratch", (2, 2, 3, D, 8, T), BF16, kind="Internal").ap()

        def tokens(a):
            return a.rearrange("b (t p) c -> b p t c", p=P)

        x_v, x1_v, x3_v, out_v = tokens(x), tokens(x1_dram), tokens(x3_dram), tokens(out)

        wh = sb("wh", [P, NW, 512], F32R)
        wl = sb("wl", [P, NW, 512], F32R)
        x_in = sb("x_in", [P, TB, C])
        x_res = sb("x_res", [P, TB, C])
        xn = sb("xn", [P, TB, C])
        xT_h = sb("xT_h", [P, KC, T], F32R)
        xT_l = sb("xT_l", [P, KC, T], F32R)
        lat_h = sb("lat_h", [P, T], F32R)
        lat_l = sb("lat_l", [P, T], F32R)
        parts = sb("parts", [P, 4, 3, T], BF16)
        rest = sb("rest", [P, 2, T])
        qs = sb("qs", [P, H, T], BF16)
        ks = sb("ks", [P, H, T], BF16)
        v_next = sb("v_next", [P, TB, H, D])
        v_sb = sb("v_sb", [P, TB, H, 32])
        probs = sb("probs", [P, P_BUFS, 512])
        y_raw = sb("y_raw", [P, 2, T])
        tok = sb("tok", [P, TB, C])
        tT_h = sb("tT_h", [P, KC, T], F32R)
        tT_l = sb("tT_l", [P, KC, T], F32R)
        x_new = sb("x_new", [P, TB, C])
        gate = sb("gate", [P, 3, KC, T])
        cell = sb("cell", [P, KC, T])
        c_h = sb("c_h", [P, KC, T], F32R)
        c_l = sb("c_l", [P, KC, T], F32R)
        c_bias = sb("c_bias", [P, TB, C])
        kv_sb = c_bias[:, 0:2, :].rearrange("p b c -> p (b c)")
        neg_max = sb("neg_max", [P, TB, H])
        m_part = [sb(f"m_part{i}", [8, 2, T // 2], BF16) for i in range(2)]
        inv = sb("inv", [P, 2, TB, 4])
        stats = sb("stats", [P, TB, 6])
        ln_t = sb("ln_t", [P, 6, TB])
        power = sb("power", [P, TB])
        ident = sb("ident", [P, P])
        ident_b = sb("ident_b", [P, P], BF16)
        neg_mask = sb("neg_mask", [P, P], BF16)
        tick = sb("tick", [1, 1 + P_BUFS])
        col = sb("col", [P, 8])
        bo_sb = sb("bo_sb", [P, C])

        ps_exp = ctx.enter_context(nc.psum_tensor("ps_exp", [P, EXP_BANKS, 512], F32))
        ps_max = ctx.enter_context(nc.psum_tensor("ps_max", [P, MAX_BANKS, 512], F32))
        ps_y = ctx.enter_context(nc.psum_tensor("ps_y", [P, 512], F32))
        ps_w = ctx.enter_context(nc.psum_tensor("ps_w", [P, 2, 512], F32))

        S = {name: sem(name) for name in RATES}
        work_full = [sem(f"work_full{i}") for i in range(2)]
        work_free = [sem(f"work_free{i}") for i in range(2)]
        zeroed, consts, ident_cast = sem("zeroed"), sem("consts"), sem("ident_cast")
        w_raw = [sem(f"w_raw{i}") for i in range(6)]
        w_high, w_low = sem("w_high"), sem("w_low")
        small_loaded, col_half = sem("small_loaded"), sem("col_half")
        c_start = sem("c_start")
        c_loaded = [sem(f"c_loaded{i}") for i in range(XC)]
        ln_c = sem("ln_c")
        high_c, tanh_c, sum_c = sem("high_c"), sem("tanh_c"), sem("sum_c")
        out_stored = [sem(f"out_stored{i}") for i in range(XC)]

        def by_tokens(a):
            return a.rearrange("p k (a c) -> p (k a) c", c=C)

        x_c = (x_in[:, :, :], x_res[:, :, :], by_tokens(y_raw[:, :, :]), by_tokens(rest[:, :, :]))
        h_c = (x_new[:, :, :],) + tuple(by_tokens(gate[:, g, :, :]) for g in range(3))
        norm_c = (xn, tok)
        turned_c = ((xT_h, xT_l), (tT_h, tT_l))

        block = ctx.enter_context(nc.Block())

        def wait(eng, ph, name, n, k):
            value = ph.val(name, n, k)
            if isinstance(value, int) and value <= 0:
                return
            eng.wait_ge(S[name], value)

        def wait_full(eng, w, use):
            eng.wait_ge(work_full[w.slot(use)], w.count(w.slot(use), w.nth(use) + 1))

        def wait_read(eng, w, *uses, bank_of=None):
            need = {}
            for use in uses:
                if bank_of and w.order.index(use) > w.order.index(bank_of):
                    need = {slot: max(need.get(slot, 0), 0) for slot in range(2)}
                    continue
                need[w.slot(use)] = max(need.get(w.slot(use), 0), w.nth(use) + 1)
            if bank_of:
                need[w.slot(bank_of)] = max(need.get(w.slot(bank_of), 0), w.nth(bank_of))
            for slot, k in need.items():
                value = w.count(slot, k)
                if not (isinstance(value, int) and value == 0):
                    eng.wait_ge(work_free[slot], value)

        def part(unit, i):
            return parts[:, unit, i if unit < 2 else 2 - i, :]

        def k_head(ph, head):
            return head - head % 8 if ph.shared else head

        pass_a, pass_b = Pass("A"), Pass("B")

        nc.disable_value_cache = True
        @block.sync
        def _(sp):
            sp.dma_start(col[:, :], cols).then_inc(small_loaded, 16)
            sp.dma_start(bo_sb[:, :], bo_rows).then_inc(small_loaded, 16)
            for i in range(NW):
                if i >= 6:
                    sp.wait_ge(w_low, i - 5)
                sp.dma_start(gate[:, (i % 6) // 2, i % 2, :], wts[i]).then_inc(w_raw[i % 6], 16)

            def load(ph, b):
                sp.dma_start(x_in[:, :, :], (x_v if ph.shared else x1_v)[b]).then_inc(S["x_loaded"], 16)

            def load_residual(ph, b):
                if not ph.shared:
                    wait(sp, ph, "x2_stored", b, 16)
                sp.dma_start(x_res[:, :, :], (x_v if ph.shared else x1_v)[b]).then_inc(S["xres_loaded"], 16)

            def store_x2(ph, n):
                wait(sp, ph, "x2_sum", n, 2)
                sp.dma_start(x1_v[n], x_in[:, :, :]).then_inc(S["x2_stored"], 16)

            def write_half(ph, n, half):
                wait(sp, ph, f"stacked{half}", n, 0)
                if ph.shared and half == 0:
                    wait(sp, ph, "stacked1", n, 0)
                for k in range(1 if ph.shared and half else 2):
                    unit = half + 2 * k
                    wait(sp, ph, "part3", n, 2 * half + k + 1)
                    heads = 1 if ph.shared and k else 8
                    for i in range(3):
                        sp.dma_start(scratch[half, k, i, :, 0:heads, :].rearrange("d g n -> g d n"),
                                     parts[0:D * heads, unit, i, :]).then_inc(S[f"written{half}"], 16)

            def stack_half(ph, n, half):
                wait(sp, ph, f"written{half}", n, 48 if ph.shared and half else 96)
                for k, (dst, runs) in enumerate(((qs, Q_RUNS), (ks, K_RUNS))):
                    heads = 1 if ph.shared and k else 8
                    for at, first, blocks in runs:
                        sp.dma_start(dst[D * at:D * (at + blocks), 8 * half:8 * half + heads, :],
                                     scratch[0 if ph.shared and k else half, k, first:first + blocks, :, 0:heads, :]
                                     .rearrange("j d g n -> (j d) g n")).then_inc(S[f"stacked{half}"], 16)

            def max_rows(ph, n, half, w, uses):
                wait_read(sp, w, *uses)
                for i in range(2):
                    sp.dma_start(qs[ROWS + i:ROWS + i + 1, 8 * half:8 * half + 8, :],
                                 m_part[i][:, :, :]).then_inc(S[f"m_loaded{half}"], 16)

            def store(ph, b, w):
                wait_read(sp, w, "o0", "o1")
                sp.dma_start((x1_v if ph.shared else x3_v)[b], x_new[:, :, :]).then_inc(S["x_stored"], 16)

            def attention(ph, b, w, first=False, last=False):
                wait(sp, ph, "ln_x", b + 1, LN_OPS)
                if not ph.shared:
                    wait(sp, ph, "ln_x2", b + 1, LN_OPS)
                    wait(sp, ph, "x2_stored", NB - 1 if last else b + 1, 16)
                load(ph, NB - 1 if last else b + 2)
                wait(sp, ph, "scores_full", b, 0)
                stack_half(ph, b, 1)
                if not first:
                    store(ph, b - 1, w)
                    load_residual(ph, b)
                write_half(ph, b + 1, 0)
                write_half(ph, b + 1, 1)
                max_rows(ph, b, 1, w, MAX1)
                wait(sp, ph, "scores_full", b, UH)
                stack_half(ph, b + 1, 0)
                if not ph.shared and not last:
                    store_x2(ph, b + 2)
                max_rows(ph, b + 1, 0, w, MAX0)

            for ph in (pass_a, pass_b):
                if ph is pass_b:
                    wait(sp, pass_a, "x_stored", NB - 1, 16)
                    wait(sp, pass_a, "ln_x", NB + 1, LN_OPS)
                for n in range(2):
                    load(ph, n)
                    if not ph.shared:
                        store_x2(ph, n)
                    if n == 0:
                        load_residual(ph, 0)
                        write_half(ph, 0, 0)
                        write_half(ph, 0, 1)
                        stack_half(ph, 0, 0)
                        wait(sp, ph, "ln_x", 0, LN_OPS)
                        if not ph.shared:
                            wait(sp, ph, "ln_x2", 0, LN_OPS)
                            wait(sp, ph, "x2_stored", 0, 16)
                max_rows(ph, 0, 0, Work(ph.name + "pro1"), MAX0)
                attention(ph, 0, Work(ph.name + "first"), first=True)
                with sp.Fori(0, NB - 3) as t:
                    attention(ph, t + 1, Work(ph.name + "body", t))
                for b in (NB - 2, NB - 1):
                    attention(ph, b, Work(ph.name + "body", b - 1), last=True)
                store(ph, NB - 1, Work(ph.name + "last"))

            wait(sp, pass_b, "x_stored", NB - 1, 16)
            wait(sp, pass_b, "ln_x2", NB + 1, LN_OPS)
            wait(sp, pass_b, "ln_a", NB - 1, LN_OPS)
            wait(sp, pass_b, "y_copied", NB - 1, 4)
            wait_read(sp, Work("Bbias"), *BIAS)
            for i in range(XC):
                sp.dma_start(x_c[i], x3_v[i]).then_inc(c_loaded[i], 16)

            def store_c(t, last=False):
                for i in range(XC):
                    sp.wait_ge(sum_c, 2 * XC * t + (2 * i + 2))
                    sp.dma_start(out_v[XC * t + i], x_c[i]).then_inc(out_stored[i], 16)
                    if not last:
                        sp.wait_ge(out_stored[i], 16 * t + 16)
                        sp.dma_start(x_c[i], x3_v[XC * t + (XC + i)]).then_inc(c_loaded[i], 16)

            with sp.Fori(0, NB // XC - 1) as t:
                store_c(t)
            store_c(NB // XC - 1, last=True)
            for i in range(XC):
                sp.wait_ge(out_stored[i], 16 * (NB // XC))
            for i in range(2):
                wait(sp, pass_b, f"written{i}", NB, 96)
            wait(sp, pass_b, "stacked0", NB, 96)
            wait(sp, pass_b, "m_loaded0", NB, 32)

        nc.disable_value_cache = False
        @block.gpsimd
        def _(pool):
            pool.memset(ident[:, :], 0.0).then_inc(zeroed, 1)
            pool.memset(neg_mask[:, :], 0.0).then_inc(zeroed, 1)
            pool.memset(tick[:, :], 0.0)
            pool.memset(power[:, :], -0.5)
            pool.memset(v_sb[:, :, :, :], 0.0).then_inc(zeroed, 1)
            pool.wait_ge(zeroed, 3)
            pool.memset(ks[ROWS:P, :, :], 1.0).then_inc(consts, 1)
            pool.wait_ge(consts, 1)
            pool.memset(v_sb[:, :, :, D:D + 1], 1.0).then_inc(consts, 1)
            pool.affine_select(out=ident[:, :], in_=ident[:, :], compare_op=ALU.not_equal, fill=1.0,
                               base=0, pattern=[[-1, P]], channel_multiplier=1).then_inc(consts, 1)
            pool.affine_select(out=neg_mask[:, :], in_=neg_mask[:, :], compare_op=ALU.is_ge, fill=NEG,
                               base=0, pattern=[[-1, P]], channel_multiplier=1).then_inc(consts, 1)
            pool.wait_ge(consts, 4)

            def third_part(ph, n, use):
                unit, at = UNIT_OF[use], ph.split.index(use)
                wait(pool, ph, "part2", n, at + 1)
                wait(pool, ph, f"written{unit % 2}", n, 0)
                pool.tensor_tensor(part(unit, 2), rest[:, at % 2, :], part(unit, 1),
                                   ALU.subtract).then_inc(S["part3"], 1)

            def mask(ph, t, u):
                heads, _, width = EXP_UNITS[u % NU]
                n = len(heads)
                wait(pool, ph, "exp_done", t, u + 1)
                at = 1 + u % P_BUFS
                pool.tensor_tensor(tick[:, at:at + 1], tick[:, 0:1], tick[:, 0:1], ALU.mult)
                pr = probs[:, u % P_BUFS, 0:n * width].rearrange("p (h n) -> p h n", h=n)[:, :, 0:P]
                pool.affine_select(out=pr, in_=pr, compare_op=ALU.is_ge, fill=0.0, base=0,
                                   pattern=[[0, n], [1, P]], channel_multiplier=-1).then_inc(S["masked"], 1)

            def rstd(s, count):
                pool.wait_ge(s, count(TB + 7))
                pool.tensor_tensor(ln_t[:, 2, :], ln_t[:, 1, :], power[:, :], ALU.pow).then_inc(s, 1)

            def rstd_of(ph, n, use):
                name = LN_COUNT[use]
                rstd(S[name], lambda k: ph.val(name, n, k))

            def attention(ph, b, table):
                for u in range(UA):
                    mask(ph, b, u)
                    for use in table.get(u + 1, []):
                        if use[:-1] in LN_COUNT:
                            rstd_of(ph, ph.round(use, b), use[:-1])
                    for use in table.get(u - 1, []):
                        if use[:-1] in ph.split:
                            third_part(ph, b + 1, use[:-1])

            for ph in (pass_a, pass_b):
                norms = [use for use in EARLY[ph.name] if use in LN_COUNT]
                for use in norms:
                    rstd_of(ph, 0, use)
                for use in ph.split:
                    third_part(ph, 0, use)
                for use in norms:
                    rstd_of(ph, 1, use)
                attention(ph, 0, ph.first)
                with pool.Fori(0, NB - 1) as t:
                    attention(ph, t + 1, ph.all)
                rstd_of(ph, NB - 1, "post")

            def out_c(t, last=False):
                for i in range(XC):
                    if not (last and i == XC - 1):
                        rstd(ln_c, lambda k: LN_OPS * XC * t + (LN_OPS * (i + 1) + k))
                    for half in range(2):
                        pool.wait_ge(tanh_c, 2 * XC * t + (2 * i + half + 1))
                        x = x_c[i][:, 2 * half:2 * half + 2, :]
                        pool.tensor_tensor(x, x, h_c[i][:, 2 * half:2 * half + 2, :], ALU.add)\
                            .then_inc(sum_c, 1)

            rstd(ln_c, lambda k: k)
            with pool.Fori(0, NB // XC - 1) as t:
                out_c(t)
            out_c(NB // XC - 1, last=True)

        @block.scalar
        def _(act):
            act.wait_ge(small_loaded, 32)
            act.activation(col[:, 0:4], col[:, 0:4], ACT.Copy, scale=0.5).then_inc(col_half, 1)
            act.activation(col[:, 6:8], col[:, 6:8], ACT.Copy, scale=2.0).then_inc(col_half, 1)
            act.wait_ge(col_half, 2)

            def copy_high(ph, w, use, dst, name):
                wait_full(act, w, use)
                act.activation(dst, ps_w[:, w.slot(use), :], ACT.Copy).then_inc(S[name], 1)

            def first_part(ph, n, w, use):
                unit = UNIT_OF[use]
                wait(act, ph, f"written{unit % 2}", n, 0)
                wait_full(act, w, use)
                if use == "kv":
                    act.activation(kv_sb, ps_w[:, w.slot(use), :], ACT.Copy).then_inc(S["kv_copied"], 1)
                act.activation(part(unit, 0), ps_w[:, w.slot(use), :], ACT.Copy,
                               scale=SCALE if unit < 2 else 1.0).then_inc(S["part1"], 1)

            def second_part(ph, w, use):
                wait_read(act, w, use)
                act.activation(part(UNIT_OF[use], 1), rest[:, ph.split.index(use) % 2, :],
                               ACT.Copy).then_inc(S["part2"], 1)

            def values(ph, n, w, use):
                i = int(use[1])
                if i == 0:
                    wait(act, ph, "v_moved", n, 0)
                wait_full(act, w, use)
                bank = ps_w[:, w.slot(use), :]
                if ph.shared:
                    src, dst = bank[:, 0:2 * P].rearrange("p (b n) -> p b n", b=2)[:, :, D:2 * D], \
                        v_next[:, 2 * i:2 * i + 2, 0, :]
                else:
                    src, dst = bank, v_next[:, 2 * i:2 * i + 2, :, :].rearrange("p b h d -> p (b h d)")
                ins = act.activation(dst, src, ACT.Copy)
                ins.then_inc(work_free[w.slot(use)], 1)

            def max_high(ph, n, w, use):
                half, i = int(use[1]), int(use[2])
                wait(act, ph, f"m_loaded{1 - half}", n, 32 if half else 0)
                wait_full(act, w, use)
                act.activation(m_part[0][:, i, :], ps_w[0:8, w.slot(use), 0:T // 2], ACT.Copy)\
                    .then_inc(S[f"m_high{half}"], 1)

            def exps(ph, t, u):
                heads, _, width = EXP_UNITS[u % NU]
                used = len(heads) * width
                wait(act, ph, "pv_done", t, freed(u, P_BUFS))
                wait(act, ph, "scores_full", t, u + 1)
                act.activation(probs[:, u % P_BUFS, 0:used], ps_exp[:, u % EXP_BANKS, 0:used], ACT.Exp)\
                    .then_inc(S["exp_done"], 1)

            def copy_y(ph, t, g):
                wait(act, ph, "pv_done", t, NU * (g + 1))
                act.activation(y_raw[:, g % 2, :], ps_y[:, :], ACT.Copy).then_inc(S["y_copied"], 1)

            def gates(ph, n, w, use):
                m, g = divmod(int(use[1]), 3)
                wait_full(act, w, use)
                act.activation(gate[:, g, m, :], ps_w[:, w.slot(use), :], ACT.Tanh,
                               bias=col[:, 2 * g + m:2 * g + m + 1], scale=0.5 if g < 2 else 1.0)\
                    .then_inc(work_free[w.slot(use)], 1)

            def step(ph, b, w, use):
                n = ph.round(use, b)
                if use in NOT_ON_ACT or use[-1] == "-" or use[0] == "y" and use[1] != "T":
                    return
                if "xT" in use:
                    copy_high(ph, w, use, xT_h[:, int(use[-1]), :], "high_e")
                elif "x2T" in use:
                    copy_high(ph, w, use, xT_h[:, int(use[-1]), :], "high_l")
                elif use == "lat":
                    copy_high(ph, w, use, lat_h[:, :], "high_l")
                elif use[1] == "T":
                    copy_high(ph, w, use, tT_h[:, int(use[-1]), :], "high_a")
                elif use[0] == "h":
                    wait_read(act, w, use)
                    h = x_new[:, 2 * int(use[1]):2 * int(use[1]) + 2, :]
                    act.activation(h, h, ACT.Tanh).then_inc(S["h_tanh"], 1)
                elif use[-1] == "+":
                    second_part(ph, w, use[:-1])
                elif use in UNIT_OF:
                    first_part(ph, n, w, use)
                elif use[0] == "v":
                    values(ph, n, w, use)
                elif use[0] == "m":
                    max_high(ph, n, w, use)
                elif use[0] == "g":
                    gates(ph, n, w, use)

            def attention(ph, b, w, table, first=False):
                for u in range(UA):
                    exps(ph, b, u)
                    if u % NU == PV_LAG - 1:
                        if u > NU:
                            copy_y(ph, b, u // NU - 1)
                        elif not first:
                            copy_y(ph, b - 1, 3)
                    for use in table.get(u, []):
                        step(ph, b, w, use)

            for ph in (pass_a, pass_b):
                for use in EARLY[ph.name]:
                    step(ph, -2, Work(ph.name + "pro0"), use)
                for use in LATE[ph.name]:
                    step(ph, -1, Work(ph.name + "pro0"), use)
                for use in EARLY[ph.name]:
                    step(ph, -1, Work(ph.name + "pro1"), use)
                for use in MAX0:
                    step(ph, -1, Work(ph.name + "pro1"), use)
                attention(ph, 0, Work(ph.name + "first"), ph.first, first=True)
                with act.Fori(0, NB - 1) as t:
                    attention(ph, t + 1, Work(ph.name + "body", t), ph.all)
                copy_y(ph, NB - 1, 3)
                for use in LAST:
                    step(ph, NB, Work(ph.name + "last"), use)

            with act.Fori(0, NB // XC) as t:
                w = Work("C", t)
                for i in range(XC):
                    for k in range(KC):
                        wait_full(act, w, f"cT{i}{k}")
                        act.activation(turned_c[i % 2][0][:, k, :], ps_w[:, w.slot(f"cT{i}{k}"), :], ACT.Copy)\
                            .then_inc(high_c, 1)
                    for half in range(2):
                        wait_read(act, w, f"ch{i}{half}")
                        h = h_c[i][:, 2 * half:2 * half + 2, :]
                        act.activation(h, h, ACT.Tanh).then_inc(tanh_c, 1)

        @block.vector
        def _(dve):
            for i in range(NW):
                dve.wait_ge(w_raw[i % 6], 16 * (i // 6 + 1))
                raw = gate[:, (i % 6) // 2, i % 2, :]
                dve.tensor_copy(wh[:, i, :], raw).then_inc(w_high, 1)
                dve.wait_ge(w_high, i + 1)
                dve.tensor_tensor(wl[:, i, :], raw, wh[:, i, :].bitcast(F32), ALU.subtract).then_inc(w_low, 1)
            dve.wait_ge(consts, 4)
            dve.tensor_copy(ident_b[:, :], ident[:, :]).then_inc(ident_cast, 1)
            dve.wait_ge(small_loaded, 32)
            dve.wait_ge(col_half, 2)

            def first_state(n):
                done = 4 * n
                dve.memset(cell[:, :, :], 0.0).then_inc(c_start, 1)
                dve.wait_ge(c_start, done + 1)
                for m in range(KC):
                    dve.tensor_scalar(cell[:, m, :], cell[:, m, :], col[:, 6 + m:7 + m], None, ALU.add)\
                        .then_inc(c_start, 1)
                dve.wait_ge(c_start, done + 3)
                dve.tensor_scalar(c_h[:, :, :], cell[:, :, :], 0.5, None, ALU.mult).then_inc(c_start, 1)
                dve.wait_ge(c_start, done + 4)
                dve.scalar_tensor_tensor(out=c_l[:, :, :], in0=cell[:, :, :], scalar=0.5,
                                         in1=c_h[:, :, :].bitcast(F32), op0=ALU.mult, op1=ALU.subtract)\
                    .then_inc(S["c_low"], 1)

            def token_sums(src, s, first=0, end=TB):
                for b in range(first, end):
                    dve.bn_stats(stats[:, b, :], src[:, b, :]).then_inc(s, 1)

            def norm_sums(s, count):
                a, v, mean = ln_t[:, 0, :], ln_t[:, 1, :], ln_t[:, 3, :]
                diff, m2 = ln_t[:, 4, :], ln_t[:, 5, :]
                dve.wait_ge(s, count(TB))
                dve.tensor_tensor(mean, stats[:, :, 1], stats[:, :, 4], ALU.add).then_inc(s, 1)
                dve.tensor_tensor(diff, stats[:, :, 1], stats[:, :, 4], ALU.subtract).then_inc(s, 1)
                dve.tensor_tensor(m2, stats[:, :, 2], stats[:, :, 5], ALU.add).then_inc(s, 1)
                dve.wait_ge(s, count(TB + 3))
                dve.scalar_tensor_tensor(out=a, in0=diff, scalar=0.25, in1=diff, op0=ALU.mult, op1=ALU.mult)\
                    .then_inc(s, 1)
                dve.tensor_scalar(v, m2, 1.0 / C, EPS, ALU.mult, ALU.add).then_inc(s, 1)
                dve.tensor_scalar(mean, mean, 0.5, None, ALU.mult).then_inc(s, 1)
                dve.wait_ge(s, count(TB + 6))
                dve.tensor_tensor(v, v, a, ALU.add).then_inc(s, 1)

            def norm_apply(src, dst, s, count):
                mean, y = ln_t[:, 3, :], ln_t[:, 2, :]
                dve.wait_ge(s, count(TB + 8))
                for b in range(TB):
                    dve.tensor_scalar(dst[:, b, :], src[:, b, :], mean[:, b:b + 1], y[:, b:b + 1],
                                      ALU.subtract, ALU.mult).then_inc(s, 1)

            def low(ph, w, use, dst, high, name, n, k):
                wait(dve, ph, name, n, k)
                dve.tensor_tensor(dst, ps_w[:, w.slot(use), :], high.bitcast(F32), ALU.subtract)\
                    .then_inc(work_free[w.slot(use)], 1)

            def take_max(ph, n, half, u):
                heads, qb, width = MAX_UNITS[u % NU]
                h0 = 8 * half + 4 * (u // NU) + heads[0]
                k = len(heads)
                wait(dve, ph, "max_full", n, half * UH + u + 1)
                dve.tensor_reduce(neg_max[:, qb, h0:h0 + k],
                                  ps_max[:, u % MAX_BANKS, 0:k * width].rearrange("p (h n) -> p h n", h=k),
                                  AX.X, ALU.max, negate=True).then_inc(S["max_taken"], 1)

            def max_low(ph, n, w, use):
                half, i = int(use[1]), int(use[2])
                wait(dve, ph, f"m_high{half}", n, i + 1)
                dve.tensor_tensor(m_part[1][:, i, :], ps_w[0:8, w.slot(use), 0:T // 2],
                                  m_part[0][:, i, :], ALU.subtract).then_inc(work_free[w.slot(use)], 1)

            def ln_x(ph, n):
                wait(dve, ph, "x_loaded", n, 16)
                token_sums(x_in, S["ln_x"])
                norm_sums(S["ln_x"], lambda k: ph.val("ln_x", n, k))

            def add_bias(ph, n, w, use, first):
                i = int(use[1])
                if i == 0 and not first:
                    wait(dve, ph, "x_stored", n - 2, 0)
                wait_full(dve, w, use)
                dve.tensor_tensor(x_new[:, 2 * i:2 * i + 2, :].rearrange("p b c -> p (b c)"),
                                  ps_w[:, w.slot(use), :],
                                  c_bias[:, 2 * i:2 * i + 2, :].rearrange("p b c -> p (b c)"), ALU.add)\
                    .then_inc(work_free[w.slot(use)], 1)

            def ln_x2(ph, n):
                for j in range(2):
                    wait(dve, ph, "h_tanh", n, j + 1)
                    part_of = x_in[:, 2 * j:2 * j + 2, :]
                    dve.tensor_tensor(part_of, part_of, x_new[:, 2 * j:2 * j + 2, :], ALU.add)\
                        .then_inc(S["x2_sum"], 1)
                wait(dve, ph, "x2_sum", n, 2)
                token_sums(x_in, S["ln_x2"])
                norm_sums(S["ln_x2"], lambda k: ph.val("ln_x2", n, k))

            def split(ph, n, w, use):
                unit, at = UNIT_OF[use], ph.split.index(use)
                wait(dve, ph, "part1", n, at + 1)
                wait(dve, ph, "part3", n, at - 1)
                dve.scalar_tensor_tensor(out=rest[:, at % 2, :], in0=ps_w[:, w.slot(use), :],
                                         scalar=SCALE if unit < 2 else 1.0, in1=part(unit, 0),
                                         op0=ALU.mult, op1=ALU.subtract)\
                    .then_inc(work_free[w.slot(use)], 1)

            def move_values(ph, n, w, g):
                if g == 0:
                    wait_read(dve, w, "v0", "v1")
                wait(dve, ph, "pv_done", n, NU * (g + 1) - UA)
                heads = slice(4 * g, 4 * g + (1 if ph.shared else 4))
                src = v_next[:, :, 0:1, :] if ph.shared else v_next[:, :, heads, :]
                dve.tensor_copy(v_sb[:, :, heads, 0:D], src).then_inc(S["v_moved"], 1)

            def normalise(ph, t, w, g):
                use = f"y{g}"
                wait_full(dve, w, use)
                bank = ps_w[:, w.slot(use), :].rearrange("p (b j d) -> p b j d", b=TB, j=4)
                dve.reciprocal(inv[:, g % 2, :, :], bank[:, :, :, D]).then_inc(S["inv_sum"], 1)
                wait(dve, ph, "inv_sum", t, g + 1)
                dve.tensor_tensor(tok[:, :, 64 * g:64 * g + 64].rearrange("p b (j d) -> p b j d", d=D),
                                  bank[:, :, :, 0:D], inv[:, g % 2, :, :].unsqueeze(3).to_broadcast([P, TB, 4, D]),
                                  ALU.mult).then_inc(work_free[w.slot(use)], 1)

            def post(ph, n, w):
                wait(dve, ph, "xres_loaded", n, 16)
                count = lambda k: ph.val("ln_a", n, k)
                for i in range(2):
                    wait_full(dve, w, f"o{i}")
                    dve.tensor_tensor(x_new[:, 2 * i:2 * i + 2, :].rearrange("p b c -> p (b c)"),
                                      ps_w[:, w.slot(f"o{i}"), :],
                                      x_res[:, 2 * i:2 * i + 2, :].rearrange("p b c -> p (b c)"), ALU.add)\
                        .then_inc(work_free[w.slot(f"o{i}")], 1)
                    wait_read(dve, w, f"o{i}")
                    token_sums(x_new, S["ln_a"], 2 * i, 2 * i + 2)
                norm_sums(S["ln_a"], count)

            def state_sum(ph, n, w, m):
                wait_read(dve, w, f"g{3 * m + 1}", f"g{3 * m + 2}")
                dve.scalar_tensor_tensor(out=gate[:, 0, m, :], in0=gate[:, 0, m, :], scalar=1.0,
                                         in1=cell[:, m, :], op0=ALU.add, op1=ALU.mult).then_inc(S["c_sum"], 1)
                dve.scalar_tensor_tensor(out=gate[:, 1, m, :], in0=gate[:, 1, m, :], scalar=1.0,
                                         in1=gate[:, 2, m, :], op0=ALU.add, op1=ALU.mult).then_inc(S["c_sum"], 1)
                wait(dve, ph, "c_sum", n, 3 * m + 2)
                dve.scalar_tensor_tensor(out=cell[:, m, :], in0=gate[:, 0, m, :], scalar=0.5,
                                         in1=gate[:, 1, m, :], op0=ALU.mult, op1=ALU.add).then_inc(S["c_sum"], 1)

            def new_state(ph, n):
                wait(dve, ph, "c_sum", n, 6)
                dve.tensor_scalar(c_h[:, :, :], cell[:, :, :], 0.5, None, ALU.mult).then_inc(S["c_new"], 1)
                wait(dve, ph, "c_new", n, 1)
                wait(dve, ph, "x_stored", n, 16)
                dve.scalar_tensor_tensor(out=c_l[:, :, :], in0=cell[:, :, :], scalar=0.5,
                                         in1=c_h[:, :, :].bitcast(F32), op0=ALU.mult, op1=ALU.subtract)\
                    .then_inc(S["c_low"], 1)

            def step(ph, b, w, use, first=False):
                n = ph.round(use, b)
                if use == "lnx":
                    ln_x(ph, n)
                elif use == "ln2":
                    ln_x2(ph, n)
                elif use in ("lnx+", "ln2+", "post+"):
                    name = LN_COUNT[use[:-1]]
                    src, dst = (x_new, tok) if use == "post+" else (x_in, xn)
                    norm_apply(src, dst, S[name], lambda k: ph.val(name, n, k))
                elif use == "post":
                    post(ph, n, w)
                elif use in ("c0", "c1"):
                    state_sum(ph, n, w, int(use[1]))
                elif use == "state":
                    new_state(ph, n)
                elif use in MOVES:
                    move_values(ph, n, w, int(use[-1]))
                elif "x2T" in use:
                    k = int(use[-1])
                    low(ph, w, use, xT_l[:, k, :], xT_h[:, k, :], "high_l", n, k + 1)
                elif "xT" in use:
                    k = int(use[-1])
                    low(ph, w, use, xT_l[:, k, :], xT_h[:, k, :], "high_e", n, k + 1)
                elif use == "lat":
                    low(ph, w, use, lat_l[:, :], lat_h[:, :], "high_l", n, 1)
                elif use[1] == "T":
                    k = int(use[-1])
                    low(ph, w, use, tT_l[:, k, :], tT_h[:, k, :], "high_a", n, k + (3 if use[0] == "s" else 1))
                elif use[0] == "y":
                    normalise(ph, n, w, int(use[1]))
                elif use[0] == "h":
                    add_bias(ph, n, w, use, first)
                elif use in UNIT_OF:
                    split(ph, n, w, use)
                elif use[0] == "m":
                    max_low(ph, n, w, use)

            def attention(ph, b, w, table):
                for u in range(UA):
                    for half, unit in max_units(ph.name, u):
                        take_max(ph, b + 1 - half, half, unit)
                    for use in table.get(u, []):
                        step(ph, b, w, use)

            first_state(0)
            dve.wait_ge(S["c_low"], 1)
            for ph in (pass_a, pass_b):
                w = Work(ph.name + "pro0")
                for use in EARLY[ph.name]:
                    step(ph, -2, w, use, first=True)
                for use in LATE[ph.name] + MOVES[:3]:
                    step(ph, -1, w, use)
                step(ph, 0, w, "move3")
                w = Work(ph.name + "pro1")
                for use in EARLY[ph.name]:
                    step(ph, -1, w, use, first=True)
                for u in range(UH):
                    take_max(ph, 0, 0, u)
                for use in MAX0:
                    step(ph, -1, w, use)
                attention(ph, 0, Work(ph.name + "first"), ph.first)
                with dve.Fori(0, NB - 1) as t:
                    attention(ph, t + 1, Work(ph.name + "body", t), ph.all)
                for use in LAST:
                    step(ph, NB, Work(ph.name + "last"), use)
                w = Work(ph.name + "bias")
                for i in range(2):
                    use = BIAS[i]
                    wait_full(dve, w, use)
                    for b in range(2):
                        ins = dve.tensor_tensor(c_bias[:, 2 * i + b, :], ps_w[:, w.slot(use), b * C:(b + 1) * C],
                                                bo_sb[:, :], ALU.add)
                    ins.then_inc(work_free[w.slot(use)], 1)
                wait_read(dve, w, *BIAS)
                if ph.shared:
                    first_state(1)

            def norm_ahead(t, i):
                dve.wait_ge(c_loaded[i % XC], 16 * t + 16 * (i // XC + 1))
                count = lambda k: LN_OPS * XC * t + (LN_OPS * i + k)
                token_sums(x_c[i % XC], ln_c)
                norm_sums(ln_c, count)
                norm_apply(x_c[i % XC], norm_c[i % 2], ln_c, count)

            def out_c(t, w, last=False):
                for i in range(XC):
                    for k in range(KC):
                        use = f"cT{i}{k}"
                        dve.wait_ge(high_c, 2 * XC * t + (2 * i + k + 1))
                        dve.tensor_tensor(turned_c[i % 2][1][:, k, :], ps_w[:, w.slot(use), :],
                                          turned_c[i % 2][0][:, k, :].bitcast(F32), ALU.subtract)\
                            .then_inc(work_free[w.slot(use)], 1)
                    if not (last and i == XC - 1):
                        norm_ahead(t, i + 1)
                    for half in range(2):
                        use = f"ch{i}{half}"
                        wait_full(dve, w, use)
                        dve.tensor_tensor(h_c[i][:, 2 * half:2 * half + 2, :],
                                          ps_w[:, w.slot(use), :].rearrange("p (b c) -> p b c", c=C),
                                          c_bias[:, 2 * half:2 * half + 2, :], ALU.add)\
                            .then_inc(work_free[w.slot(use)], 1)

            norm_ahead(0, 0)
            with dve.Fori(0, NB // XC - 1) as t:
                out_c(t, Work("C", t))
            out_c(NB // XC - 1, Work("C", NB // XC - 1), last=True)

        @block.tensor
        def _(pe):
            pe.wait_ge(consts, 4)
            pe.wait_ge(ident_cast, 1)
            pe.wait_ge(w_low, NW)

            def exact(dst, terms, first=True, last=True):
                n = 3 * len(terms)
                i = 0
                for lh, ll, rh, rl in terms:
                    for a, b in ((lh, rh), (lh, rl), (ll, rh)):
                        ins = pe.matmul(dst, a, b, start=first and i == 0, stop=last and i == n - 1)
                        i += 1
                return ins

            def claim(w, use, *made):
                wait_read(pe, w, *made, bank_of=use)
                return ps_w[:, w.slot(use), :]

            def filled(ins, w, use):
                ins.then_inc(work_full[w.slot(use)], 1)

            def turn(w, use, src, k, *made):
                bank = claim(w, use, *made)
                for b in range(TB):
                    ins = pe.transpose(bank[:, b * P:(b + 1) * P], src[:, b, k * P:(k + 1) * P], ident[:, :])
                filled(ins, w, use)

            def by_token(w, use, i, hi, lo, tile, *made):
                bank = claim(w, use, *made)
                for b in range(2):
                    blk = slice((2 * i + b) * P, (2 * i + b + 1) * P)
                    ins = exact(bank[:, b * C:(b + 1) * C],
                                [(hi[:, k, blk], lo[:, k, blk], wh[:, tile, k * C:(k + 1) * C],
                                  wl[:, tile, k * C:(k + 1) * C]) for k in range(KC)])
                filled(ins, w, use)

            def by_width(w, use, m, tile, hi, lo, bank, first=True, last=True):
                cut = [slice(k * C + m * P, k * C + m * P + P) for k in range(KC)]
                return exact(bank, [(wh[:, tile, cut[k]], wl[:, tile, cut[k]], hi[:, k, :], lo[:, k, :])
                                    for k in range(KC)], first, last)

            def parts_of_x(ph, n, w, use):
                if ph.shared:
                    cut, made = {"lat": (0, ("xT0", "xT1")), "q0": (2 * P, ("lat",)), "q1": (3 * P, ("lat",)),
                                 "kv": (0, ("lat",))}[use]
                    tile = W_KV if use == "kv" else W_DOWN_Q
                    if use == "lat":
                        bank = claim(w, use, *made)
                        ins = exact(bank, [(wh[:, tile, k * P:(k + 1) * P], wl[:, tile, k * P:(k + 1) * P],
                                            xT_h[:, k, :], xT_l[:, k, :]) for k in range(KC)])
                    else:
                        bank = claim(w, use, *made)
                        ins = exact(bank, [(wh[:, tile, cut:cut + P], wl[:, tile, cut:cut + P],
                                            lat_h[:, :], lat_l[:, :])])
                else:
                    bank = claim(w, use, "x2T0", "x2T1")
                    ins = by_width(w, use, int(use[1]), W_BQ if use[0] == "q" else W_BK, xT_h, xT_l, bank)
                filled(ins, w, use)

            def values(ph, n, w, use):
                i = int(use[1])
                if ph.shared:
                    wait(pe, ph, "kv_copied", n, 1)
                    bank = claim(w, use)
                    for b in range(2):
                        blk = slice((2 * i + b) * P, (2 * i + b + 1) * P)
                        ins = pe.transpose(bank[:, b * P:(b + 1) * P], kv_sb[:, blk], ident[:, :])
                    filled(ins, w, use)
                else:
                    by_token(w, use, i, xT_h, xT_l, W_BV)

            def scores_max(ph, n, half, u):
                heads, qb, width = MAX_UNITS[u % NU]
                if u == 0:
                    wait(pe, ph, f"stacked{half}", n, 96)
                wait(pe, ph, "max_taken", n, half * UH + u - MAX_BANKS + 1)
                for i, j in enumerate(heads):
                    head = 8 * half + 4 * (u // NU) + j
                    bank = ps_max[:, u % MAX_BANKS, i * width:(i + 1) * width]
                    pe.matmul(bank, qs[0:ROWS, head, qb * P:(qb + 1) * P],
                              ks[0:ROWS, k_head(ph, head), 0:width], start=True, stop=False)
                    ins = pe.matmul(bank[:, width - P:width], ident_b[:, :], neg_mask[:, :], start=False, stop=True)
                ins.then_inc(S["max_full"], 1)

            def max_turn(ph, n, w, use):
                half, i = int(use[1]), int(use[2])
                wait(pe, ph, "max_taken", n, half * UH + UH)
                bank = claim(w, use)
                for b in range(2):
                    ins = pe.transpose(bank[0:8, b * P:(b + 1) * P],
                                       neg_max[:, 2 * i + b, 8 * half:8 * half + 8], ident[:, :])
                filled(ins, w, use)

            def scores_exp(ph, t, u):
                heads, kb, width = EXP_UNITS[u % NU]
                if u == 0:
                    wait(pe, ph, "m_loaded0", t, 32)
                if u == UH:
                    wait(pe, ph, "m_loaded1", t, 32)
                wait(pe, ph, "exp_done", t, freed(u, EXP_BANKS))
                for i, j in enumerate(heads):
                    head = 4 * (u // NU) + j
                    ins = pe.matmul(ps_exp[:, u % EXP_BANKS, i * width:(i + 1) * width],
                                    ks[0:STACK, k_head(ph, head), kb * P:(kb + 1) * P],
                                    qs[0:STACK, head, T - width:T], start=True, stop=True)
                ins.then_inc(S["scores_full"], 1)

            def product(ph, t, u):
                g = u // NU
                heads, kb, width = EXP_UNITS[u % NU]
                if u % NU == 0:
                    wait(pe, ph, "y_copied", t, g)
                    wait(pe, ph, "v_moved", t, g + 1)
                wait(pe, ph, "masked", t, u + 1)
                for i, j in enumerate(heads):
                    head = 4 * g if ph.shared else 4 * g + j
                    ins = pe.matmul(ps_y[32 * j:32 * j + 32, T - width:T], v_sb[:, kb, head, :],
                                    probs[:, u % P_BUFS, i * width:(i + 1) * width],
                                    start=(kb == 0), stop=(kb == TB - 1))
                ins.then_inc(S["pv_done"], 1)

            def turn_y(ph, t, w, g):
                use = f"y{g}"
                wait(pe, ph, "y_copied", t, g + 1)
                bank = claim(w, use)
                for b in range(TB):
                    ins = pe.transpose(bank[:, b * P:(b + 1) * P], y_raw[:, g % 2, b * P:(b + 1) * P], ident[:, :])
                filled(ins, w, use)

            def step(ph, b, w, use):
                n = ph.round(use, b)
                if use in MOVES + ["post", "lnx", "ln2", "c0", "c1", "state"] or use[-1] == "+":
                    return
                if "T" in use:
                    made = ()
                    if use == "xT0":
                        wait(pe, ph, "ln_x", n, LN_OPS)
                    elif use == "x2T0":
                        wait(pe, ph, "ln_x2", n, LN_OPS)
                    elif use == "sT0":
                        wait(pe, ph, "ln_a", n, LN_OPS)
                    elif use == "yT0":
                        made = ("y3",)
                    turn(w, use, xn if use[0] == "x" else tok, int(use[-1]), *made)
                elif use[0] == "y":
                    turn_y(ph, n, w, int(use[1]))
                elif use[0] == "h":
                    by_token(w, use, int(use[1]), xT_h, xT_l, W_O, "xT0", "xT1")
                elif use[0] == "o":
                    by_token(w, use, int(use[1]), tT_h, tT_l, W_PROJ if ph.shared else W_BO, "yT0", "yT1")
                elif use[0] == "v":
                    values(ph, n, w, use)
                elif use[0] == "m":
                    max_turn(ph, n, w, use)
                elif use[0] == "g":
                    m, g = divmod(int(use[1]), 3)
                    if use[-1] == "-":
                        bank = claim(w, use[:2], "sT0", "sT1")
                        by_width(w, use, m, GATES[g][0], tT_h, tT_l, bank, True, False)
                    else:
                        if use == "g0":
                            wait(pe, ph, "c_low", n, 0)
                        filled(by_width(w, use, m, GATES[g][1], c_h, c_l, ps_w[:, w.slot(use), :], False, True),
                               w, use)
                else:
                    parts_of_x(ph, n, w, use)

            def attention(ph, b, w, table, first=False):
                for u in range(UA):
                    scores_exp(ph, b, u)
                    if u >= PV_LAG:
                        product(ph, b, u - PV_LAG)
                    elif not first:
                        product(ph, b - 1, UA + u - PV_LAG)
                    for half, unit in max_units(ph.name, u):
                        scores_max(ph, b + 1 - half, half, unit)
                    for use in table.get(u, []):
                        step(ph, b, w, use)

            for ph in (pass_a, pass_b):
                w = Work(ph.name + "pro0")
                for use in EARLY[ph.name]:
                    step(ph, -2, w, use)
                for use in LATE[ph.name]:
                    step(ph, -1, w, use)
                w = Work(ph.name + "pro1")
                for use in EARLY[ph.name]:
                    step(ph, -1, w, use)
                for u in range(UH):
                    scores_max(ph, 0, 0, u)
                for use in MAX0:
                    step(ph, -1, w, use)
                attention(ph, 0, Work(ph.name + "first"), ph.first, first=True)
                with pe.Fori(0, NB - 1) as t:
                    attention(ph, t + 1, Work(ph.name + "body", t), ph.all)
                for u in range(UA - PV_LAG, UA):
                    product(ph, NB - 1, u)
                for use in LAST:
                    step(ph, NB, Work(ph.name + "last"), use)
                w = Work(ph.name + "bias")
                wait(pe, ph, "c_low", NB - 1, 1)
                for i, use in enumerate(BIAS):
                    by_token(w, use, i, c_h, c_l, U_O)
                wait_read(pe, w, *BIAS)

            with pe.Fori(0, NB // XC) as t:
                w = Work("C", t)
                for i in range(XC):
                    pe.wait_ge(ln_c, LN_OPS * XC * t + LN_OPS * (i + 1))
                    for k in range(KC):
                        turn(w, f"cT{i}{k}", norm_c[i % 2], k)
                    for half in range(2):
                        by_token(w, f"ch{i}{half}", half, turned_c[i % 2][0], turned_c[i % 2][1], W_O,
                                 f"cT{i}0", f"cT{i}1")


def kernel(**inputs):
    import numpy as np
    import concourse.bacc as bacc
    from concourse.bass_utils import run_bass_kernel_spmd

    def get(name):
        return np.asarray(inputs["L0_" + name])

    def tile(w):
        return w.reshape(KC, P, C).transpose(1, 0, 2).reshape(P, KC * C)

    wts = np.zeros((NW, P, 512), np.float32)
    wts[W_DOWN_Q, :, 0:2 * P] = get("attn_a_Wc_down").reshape(KC, P, P).transpose(1, 0, 2).reshape(P, 2 * P)
    wts[W_DOWN_Q, :, 2 * P:] = get("attn_a_Wq_up")
    wts[W_KV, :, 0:2 * D] = get("attn_a_Wkv_up")
    wts[W_PROJ] = tile(get("attn_a_Wc_proj"))
    for at, name in ((W_F, "ffn_wf"), (U_F, "ffn_uf"), (W_I, "ffn_wi"), (U_I, "ffn_ui"), (W_G, "ffn_wc"),
                     (U_G, "ffn_uc"), (W_O, "ffn_wo"), (U_O, "ffn_uo"), (W_BQ, "attn_b_Wq"), (W_BK, "attn_b_Wk"),
                     (W_BV, "attn_b_Wv"), (W_BO, "attn_b_Wo")):
        wts[at] = tile(get(name).T)
    cols = np.zeros((P, 8), np.float32)
    for i, name in enumerate(("ffn_bf", "ffn_bi", "ffn_bc", "ffn_in_c")):
        cols[:, 2 * i:2 * i + 2] = get(name).reshape(KC, P).T
    arrays = {
        "x": np.ascontiguousarray(get("attn_a_x")),
        "wts": wts,
        "cols": cols,
        "bo_rows": np.ascontiguousarray(np.broadcast_to(get("ffn_bo"), (P, C))),
    }
    nc = bacc.Bacc("TRN2", target_bir_lowering=False, num_devices=1)
    args = [nc.dram_tensor(name, a.shape, F32, kind="ExternalInput").ap() for name, a in arrays.items()]
    result = nc.dram_tensor("result", (NB, T, C), F32, kind="ExternalOutput").ap()
    build(nc, *args, result)
    r = run_bass_kernel_spmd(nc, [arrays], core_ids=[0])
    return r.results[0]["result"]
```
